# Optimizing a Trainium2 kernel written in Bass

```python
import numpy as np
import jax
import jax.numpy as jnp

def _softmax(x, axis=-1):
    return jax.nn.softmax(x, axis=axis)

def _gelu(x):
    return jax.nn.gelu(x, approximate=True)

def _silu(x):
    return jax.nn.silu(x)

def _sigmoid(x):
    return jax.nn.sigmoid(x)

def _layernorm(x, axis=-1, eps=1e-05):
    m = jnp.mean(x, axis=axis, keepdims=True)
    v = jnp.var(x, axis=axis, keepdims=True)
    return (x - m) / jnp.sqrt(v + eps)

def _scatter_add(tgt, idx, src, axis=0):
    return tgt.at[idx].add(src)

def _segment_sum(src, seg, n):
    return jax.ops.segment_sum(src, seg, n)
kernel_name = 'mk_adj_preln_d1_adj_r2_991401'

def setup_inputs(seed: int=0):
    np.random.seed(seed)
    _w = jnp.asarray

    def _rec_inputs():
        import jax
        import jax.numpy as jnp
        _gk = jax.random.key(seed)
        x = -0.0002928 + 1 * jax.random.normal(jax.random.fold_in(_gk, 1), (128, 128, 256), jnp.float32)
        _a = jax.random.bernoulli(jax.random.fold_in(_gk, 2), 0.03125, (128, 128, 128))
        adj = _a.astype(jnp.int32)
        return (x, adj)
    x, adj = _rec_inputs()

    def _L0_gnn_setup():
        import jax, jax.numpy as jnp
        import numpy as np
        L = 3
        D = 256
        B, N = (8, 512)
        EPS = 1e-05

        def layernorm(x, gamma, beta):
            mu = jnp.mean(x, axis=-1, keepdims=True)
            var = jnp.var(x, axis=-1, keepdims=True)
            return (x - mu) * jax.lax.rsqrt(var + EPS) * gamma + beta
        key = jax.random.key(seed)
        ks = jax.random.split(key, 12)
        s = 1.0 / np.sqrt(D)
        node_features = jax.random.normal(ks[0], (B, N, D), dtype=jnp.float32)
        adjacency_matrix = jax.random.randint(ks[1], (B, N, N), 0, 2, dtype=jnp.int32)
        return {'node_features': node_features, 'adjacency_matrix': adjacency_matrix, 'attn_w': jax.random.normal(ks[2], (L, 2 * D), dtype=jnp.float32) * (1.0 / np.sqrt(2 * D)), 'attn_b': jax.random.normal(ks[3], (L,), dtype=jnp.float32) * 0.01, 'W1': jax.random.normal(ks[4], (L, D, 4 * D), dtype=jnp.float32) * s, 'b1': jnp.zeros((L, 4 * D), dtype=jnp.float32), 'W2': jax.random.normal(ks[5], (L, 4 * D, D), dtype=jnp.float32) * (1.0 / np.sqrt(4 * D)), 'b2': jnp.zeros((L, D), dtype=jnp.float32), 'g1': jnp.ones((L, D), dtype=jnp.float32), 'beta1': jnp.zeros((L, D), dtype=jnp.float32), 'g2': jnp.ones((L, D), dtype=jnp.float32), 'beta2': jnp.zeros((L, D), dtype=jnp.float32)}
    _L0_gnn_all = _L0_gnn_setup()
    _L0_gnn_in = {k: v for k, v in _L0_gnn_all.items() if k in ('attn_w', 'attn_b', 'W1', 'b1', 'W2', 'b2', 'g1', 'beta1', 'g2', 'beta2')}
    del _L0_gnn_all
    return {'x': x, 'adj': adj, 'L0_gnn_attn_w': _L0_gnn_in['attn_w'], 'L0_gnn_attn_b': _L0_gnn_in['attn_b'], 'L0_gnn_W1': _L0_gnn_in['W1'], 'L0_gnn_b1': _L0_gnn_in['b1'], 'L0_gnn_W2': _L0_gnn_in['W2'], 'L0_gnn_b2': _L0_gnn_in['b2'], 'L0_gnn_g1': _L0_gnn_in['g1'], 'L0_gnn_beta1': _L0_gnn_in['beta1'], 'L0_gnn_g2': _L0_gnn_in['g2'], 'L0_gnn_beta2': _L0_gnn_in['beta2']}

def reference(x, adj, L0_gnn_attn_w, L0_gnn_attn_b, L0_gnn_W1, L0_gnn_b1, L0_gnn_W2, L0_gnn_b2, L0_gnn_g1, L0_gnn_beta1, L0_gnn_g2, L0_gnn_beta2):
    import jax
    import jax.numpy as jnp

    def _L0_gnn_ref(node_features, adjacency_matrix, attn_w, attn_b, W1, b1, W2, b2, g1, beta1, g2, beta2):
        import jax, jax.numpy as jnp
        import numpy as np
        L = 3
        D = 256
        B, N = (8, 512)
        EPS = 1e-05

        def layernorm(x, gamma, beta):
            mu = jnp.mean(x, axis=-1, keepdims=True)
            var = jnp.var(x, axis=-1, keepdims=True)
            return (x - mu) * jax.lax.rsqrt(var + EPS) * gamma + beta
        n = adjacency_matrix.shape[-1]
        mask = adjacency_matrix.astype(jnp.float32) + jnp.eye(n, dtype=jnp.float32) > 0
        x = node_features
        d = x.shape[-1]
        for l in range(attn_w.shape[0]):
            si = x @ attn_w[l, :d]
            sj = x @ attn_w[l, d:]
            scores = si[:, :, None] + sj[:, None, :] + attn_b[l]
            scores = jnp.where(scores >= 0, scores, 0.2 * scores)
            scores = jnp.where(mask, scores, -jnp.inf)
            attn = jax.nn.softmax(scores, axis=-1)
            agg = jnp.einsum('bij,bjd->bid', attn, x)
            h = layernorm(x + agg, g1[l], beta1[l])
            ff = jax.nn.gelu(h @ W1[l] + b1[l], approximate=False) @ W2[l] + b2[l]
            x = layernorm(h + ff, g2[l], beta2[l])
        return x
    h = jnp.maximum(_layernorm(x, axis=-1), 0.0)
    x = x + _L0_gnn_ref(h, adj, L0_gnn_attn_w, L0_gnn_attn_b, L0_gnn_W1, L0_gnn_b1, L0_gnn_W2, L0_gnn_b2, L0_gnn_g1, L0_gnn_beta1, L0_gnn_g2, L0_gnn_beta2)
    return x

_drawn_inputs = setup_inputs


def setup_inputs(seed=0):
    import zlib

    import numpy as np

    out = dict(_drawn_inputs(seed))
    spreads = {'L0_gnn_b1': (0.0, 0.1),
     'L0_gnn_b2': (0.0, 0.1),
     'L0_gnn_g1': (1.0, 0.2),
     'L0_gnn_beta1': (0.0, 0.1),
     'L0_gnn_g2': (1.0, 0.2),
     'L0_gnn_beta2': (0.0, 0.1)}
    factors = {'L0_gnn_attn_b': 64.0}
    for name, (base, spread) in spreads.items():
        noise = np.random.default_rng([zlib.crc32(name.encode()), seed]).standard_normal(out[name].shape)
        drawn = base * np.exp(spread * noise) if base else spread * noise
        out[name] = jnp.asarray(drawn.astype(out[name].dtype))
    for name, factor in factors.items():
        out[name] = (out[name] * factor).astype(out[name].dtype)
    return out
```

```python
from contextlib import ExitStack

import numpy as np

import concourse.bass as bass
from concourse import mybir

ALU = mybir.AluOpType
ACT = mybir.ActivationFunctionType
AX = mybir.AxisListType
F32 = mybir.dt.float32
F16 = mybir.dt.float16
BF16 = mybir.dt.bfloat16
I32 = mybir.dt.int32

P = 128
B, N, D = 128, 128, 256
L = 3
H = 4 * D
T = 4
G = B // T
RING = 4
PER = RING * L
ITEMS = G * L
KD = D // P
C = H // P
TN = T * N
EPS = 1e-5
SLOPE = 0.2
MASKED = -1e30
WSCALE = 64.0
PF_RING, G32_RING, GS_RING = 3, 3, 4
FIRST_LOOP_SLOT = 4
LOOPS = ITEMS // PER - 1


def layer_of(s):
    return (s % PER) // RING


def total(r, s, per, n):
    if isinstance(r, int):
        v = per * (PER * r + s) + n
        assert v > 0
        return v
    assert per * s + n > 0
    return r * (PER * per) + (per * s + n)


def group_total(r, s, per, n):
    g = RING * (s // PER) + s % PER
    if isinstance(r, int):
        v = per * (RING * r + g) + n
        assert v > 0
        return v
    assert per * g + n > 0
    return r * (RING * per) + (per * g + n)


def lane_total(r, s):
    g = RING * (s // PER) + s % PER
    if isinstance(r, int):
        return 16 * ((RING * r + g) // 2 + 1)
    return r * (RING // 2 * 16) + 16 * (g // 2 + 1)


def x_total(r, s, n):
    v = 2 * s + RING * (s // PER) + max(0, s % PER - (PER - RING)) + n
    return (2 * PER + RING) * r + v if isinstance(r, int) else r * (2 * PER + RING) + v


def is_item(r, s):
    return not isinstance(r, int) or 0 <= PER * r + s < ITEMS


def later(r, s, m=1):
    return not isinstance(r, int) or PER * r + s - m >= 0


def in_ring(s, c, ring):
    assert PER * C % ring == 0
    return (s * C + c) % ring


def stored_total(r, q):
    return 16 * ((RING * r + q) // 2) if isinstance(r, int) else r * (8 * RING) + 16 * (q // 2)


def slots(eng, slot):
    for s in range(-3, FIRST_LOOP_SLOT):
        slot(0, s)
    with eng.Fori(0, LOOPS) as r:
        for s in range(FIRST_LOOP_SLOT, FIRST_LOOP_SLOT + PER):
            slot(r, s)
    for s in range(FIRST_LOOP_SLOT, PER + 1):
        slot(LOOPS, s)


def gnn_kernel(nc, x, adj, attn_w, attn_b, W1, b1, W2, b2, g1, beta1, g2, beta2, out):
    with ExitStack() as ctx:
        def sb(name, shape, dt=F32):
            return ctx.enter_context(nc.sbuf_tensor(name, shape, dt))

        def ps(name, shape):
            return ctx.enter_context(nc.psum_tensor(name, shape, F32))

        def sem(name):
            return ctx.enter_context(nc.semaphore(name))

        ident = sb("ident", [P, P])
        eye_i = sb("eye_i", [P, N], I32)
        minus_half = sb("minus_half", [P, T])
        w1_f32 = sb("w1_f32", [P, KD, H])
        w2_f32 = sb("w2_f32", [P, C, D])
        w1_hi = [sb(f"w1_hi{l}", [P, KD, H], F16) for l in range(L)]
        w1_lo = [sb(f"w1_lo{l}", [P, KD, H], F16) for l in range(L)]
        w2_hi = [sb(f"w2_hi{l}", [P, C, D], F16) for l in range(L)]
        w2_lo = [sb(f"w2_lo{l}", [P, C, D], F16) for l in range(L)]
        b1_col = sb("b1_col", [P, L, C])
        g1_col = sb("g1_col", [P, L, KD])
        beta1_col = sb("beta1_col", [P, L, KD])
        attn_rows = sb("attn_rows", [P, L, 2, D])
        attn_b_col = sb("attn_b_col", [P, L])
        g1_rows = sb("g1_rows", [P, L, D])
        b2_rows = sb("b2_rows", [P, L, D])
        res_rows = sb("res_rows", [P, L, D])
        g2_rows = sb("g2_rows", [P, L, D])
        beta2_rows = sb("beta2_rows", [P, L, D])

        x_in = [sb(f"x_in{i}", [P, T, D]) for i in range(2)]
        adj_in = [sb(f"adj_in{i}", [P, T, N], I32) for i in range(2)]
        x_again = [sb(f"x_again{i}", [P, T, D]) for i in range(2)]
        y_out = [sb(f"y_out{i}", [P, T, D]) for i in range(2)]
        X = [sb(f"X{i}", [P, T, D]) for i in range(RING)]
        mask = [sb(f"mask{i}", [P, T, N], BF16) for i in range(RING)]

        s_i = [sb(f"s_i{i}", [P, T]) for i in range(RING)]
        s_j = [sb(f"s_j{i}", [P, T]) for i in range(RING)]
        dots = sb("dots", [P, 2 * T, D], BF16)
        scores = sb("scores", [P, T, N])
        leaky = sb("leaky", [P, T, N])
        row_max = sb("row_max", [P, T])
        probs = sb("probs", [P, T, N])
        row_sum = sb("row_sum", [P, T])
        row_inv = sb("row_inv", [P, T])
        probs_T = sb("probs_T", [P, TN])
        res1 = sb("res1", [P, T, D])
        norm1 = sb("norm1", [P, T, D])
        h_res = [sb(f"h_res{i}", [P, T, D]) for i in range(2)]
        hT = sb("hT", [P, KD, TN])
        hT_hi = [sb(f"hT_hi{i}", [P, KD, TN], F16) for i in range(2)]
        hT_lo = [sb(f"hT_lo{i}", [P, KD, TN], F16) for i in range(2)]
        g32 = [sb(f"g32_{i}", [P, TN]) for i in range(G32_RING)]
        g_hi = [sb(f"g_hi{i}", [P, TN], F16) for i in range(GS_RING)]
        g_lo = [sb(f"g_lo{i}", [P, TN], F16) for i in range(GS_RING)]
        res2 = sb("res2", [P, T, D])
        norm2 = sb("norm2", [P, T, D])
        bn = [sb(f"bn{i}", [P, T, 6]) for i in range(3)]
        mv = [sb(f"mv{i}", [P, T, 2]) for i in range(3)]
        var_eps = [sb(f"var_eps{i}", [P, T]) for i in range(3)]
        minus_mean = [sb(f"minus_mean{i}", [P, T]) for i in range(3)]
        rstd = [sb(f"rstd{i}", [P, T]) for i in range(3)]
        shift = [sb(f"shift{i}", [P, T]) for i in range(3)]

        p_hid = [ps(f"p_hid{i}", [P, TN]) for i in range(PF_RING)]
        p_ff = [ps(f"p_ff{i}", [P, 2, D]) for i in range(2)]
        p_att = ps("p_att", [P, T, N])
        p_mid = [ps(f"p_mid{i}", [P, 512]) for i in range(2)]

        const_dma = sem("const_dma")
        w_dma = [sem("w1_dma"), sem("w2_dma")]
        const_steps = sem("const_steps")
        pool_steps = sem("pool_steps")
        w_hi_ready, w_ready = sem("w_hi_ready"), sem("w_ready")
        x_loaded = [sem(f"x_loaded{i}") for i in range(2)]
        adj_loaded = [sem(f"adj_loaded{i}") for i in range(2)]
        x_again_loaded = [sem(f"x_again_loaded{i}") for i in range(2)]
        stored = [sem(f"stored{i}") for i in range(2)]
        mask_steps = sem("mask_steps")
        x0_ready = sem("x0_ready")
        dots_ready = sem("dots_ready")
        sj_rows_ready = sem("sj_rows_ready")
        score_steps = sem("score_steps")
        probs_ready = sem("probs_ready")
        sum_steps = sem("sum_steps")
        pT_psum = sem("pT_psum")
        pT_ready = sem("pT_ready")
        agg_ready = sem("agg_ready")
        res1_ready = sem("res1_ready")
        stat_steps = [sem(f"stat_steps{i}") for i in range(3)]
        rstd_ready = [sem(f"rstd_ready{i}") for i in range(3)]
        norm1_ready = sem("norm1_ready")
        nT_psum = sem("nT_psum")
        hT_ready = sem("hT_ready")
        hT_hi_ready = sem("hT_hi_ready")
        hT_lo_ready = sem("hT_lo_ready")
        h_res_steps = sem("h_res_steps")
        hid_psum = sem("hid_psum")
        gelu_ready = sem("gelu_ready")
        g_hi_ready = sem("g_hi_ready")
        g_lo_ready = sem("g_lo_ready")
        ff_done = sem("ff_done")
        res2_ready = sem("res2_ready")
        norm2_ready = sem("norm2_ready")
        x_steps = sem("x_steps")

        block = ctx.enter_context(nc.Block())
        CONSTS = 10 * 16

        @block.sync
        def _(sp):
            with nc.allow_non_contiguous_dma("columns of small vectors"):
                for dst, src in (
                    (b1_col[:], b1.rearrange("l (c p) -> p l c", p=P)),
                    (g1_col[:], g1.rearrange("l (c p) -> p l c", p=P)),
                    (beta1_col[:], beta1.rearrange("l (c p) -> p l c", p=P)),
                ):
                    sp.dma_start(dst, src).then_inc(const_dma, 16)
            for dst, src in (
                (attn_rows[:].rearrange("p l a d -> p (l a d)"), attn_w.rearrange("l e -> (l e)")),
                (attn_b_col[:], attn_b),
                (g1_rows[:].rearrange("p l d -> p (l d)"), g1.rearrange("l d -> (l d)")),
                (b2_rows[:].rearrange("p l d -> p (l d)"), b2.rearrange("l d -> (l d)")),
                (res_rows[:].rearrange("p l d -> p (l d)"), beta1.rearrange("l d -> (l d)")),
                (g2_rows[:].rearrange("p l d -> p (l d)"), g2.rearrange("l d -> (l d)")),
                (beta2_rows[:].rearrange("p l d -> p (l d)"), beta2.rearrange("l d -> (l d)")),
            ):
                sp.dma_start(dst, src.partition_broadcast(P)).then_inc(const_dma, 16)

            def weights(l):
                if l >= 1:
                    sp.wait_ge(w_ready, 2 * l - 1)
                sp.dma_start(w1_f32[:], W1[l].rearrange("(k p) h -> p k h", p=P)).then_inc(w_dma[0], 16)
                if l >= 1:
                    sp.wait_ge(w_ready, 2 * l)
                sp.dma_start(w2_f32[:], W2[l].rearrange("(c p) d -> p c d", p=P)).then_inc(w_dma[1], 16)

            def graphs(tensor, g):
                v = tensor.rearrange("(g t) n d -> n g t d", t=T)
                if isinstance(g, int):
                    return v[:, g]
                return v[:, bass.ds(g, 1)].rearrange("n g t d -> n (g t) d")

            def load_x(g, i):
                sp.dma_start(x_in[i][:], graphs(x, g)).then_inc(x_loaded[i], 16)

            def load_adj(g, i):
                sp.dma_start(adj_in[i][:], graphs(adj, g)).then_inc(adj_loaded[i], 16)

            def load_again(g, i):
                sp.dma_start(x_again[i][:], graphs(x, g)).then_inc(x_again_loaded[i], 16)

            def store(g, i):
                sp.dma_start(graphs(out, g), y_out[i][:]).then_inc(stored[i], 16)

            for g in range(2):
                load_x(g, g)
                load_adj(g, g)
            weights(0)
            for g in (2, 3):
                sp.wait_ge(x0_ready, 4 * (g - 1))
                load_x(g, g % 2)
                sp.wait_ge(mask_steps, 2 * (g - 1))
                load_adj(g, g % 2)
                weights(g - 1)
            load_again(0, 0)
            load_again(1, 1)
            with sp.Fori(0, LOOPS) as r:
                for q in range(RING):
                    i, g = q % 2, r * RING + q
                    sp.wait_ge(x0_ready, r * (4 * RING) + 4 * (RING + q - 1))
                    load_x(g + RING, i)
                    sp.wait_ge(mask_steps, r * (2 * RING) + 2 * (RING + q - 1))
                    load_adj(g + RING, i)
                    sp.wait_ge(x_steps, x_total(r, 2 * RING + q, 3))
                    store(g, i)
                    load_again(g + 2, i)
            for q in range(RING):
                sp.wait_ge(x_steps, x_total(LOOPS, 2 * RING + q, 3))
                store(RING * LOOPS + q, q % 2)
                if q < 2:
                    load_again(RING * LOOPS + q + 2, q % 2)
            for i in range(2):
                sp.wait_ge(stored[i], 16 * G // 2)

        @block.tensor
        def _(pe):
            def hidden(r, s, c):
                l, i = layer_of(s), s % 2
                if c == 0:
                    pe.wait_ge(hT_hi_ready, total(r, s, 1, 1))
                    pe.wait_ge(hT_lo_ready, total(r, s, 1, 1))
                if later(r, s) or c >= PF_RING:
                    pe.wait_ge(gelu_ready, total(r, s, C, c + 1 - PF_RING))
                cols = slice(c * P, (c + 1) * P)
                for n, (k, w, h) in enumerate((k, w, h) for k in range(KD) for w, h in
                                              ((w1_hi, hT_hi), (w1_hi, hT_lo), (w1_lo, hT_hi))):
                    mm = pe.matmul(p_hid[in_ring(s, c, PF_RING)][:], w[l][:, k, cols], h[i][:, k, :],
                                   start=(n == 0), stop=(n == 3 * KD - 1))
                mm.then_inc(hid_psum, 1)

            def feed(r, s, c):
                l, i = layer_of(s), c % GS_RING
                if c == 0 and later(r, s):
                    pe.wait_ge(res2_ready, total(r, s - 1, 2, 2))
                pe.wait_ge(g_hi_ready, total(r, s, C, c + 1))
                pe.wait_ge(g_lo_ready, total(r, s, C, c + 1))
                for t in range(T):
                    nodes = slice(t * N, (t + 1) * N)
                    for n, (g, w) in enumerate(((g_hi, w2_hi), (g_hi, w2_lo), (g_lo, w2_hi))):
                        mm = pe.matmul(p_ff[t // 2][:, t % 2, :], g[i][:, nodes], w[l][:, c, :],
                                       start=(c == 0 and t % 2 == 0 and n == 0),
                                       stop=(c == C - 1 and n == 2), skip_group_check=True)
                mm.then_inc(ff_done, 1)

            def spread_sj(r, s):
                pe.wait_ge(dots_ready, total(r, s, 8, 8))
                if later(r, s):
                    pe.wait_ge(pT_ready, total(r, s - 1, 1, 1))
                for t in range(T):
                    mm = pe.transpose(p_att[:, t, :], s_j[s % RING][:, t:t + 1].broadcast_to([P, P]), ident[:])
                mm.then_inc(sj_rows_ready, 1)

            def transpose_probs(r, s):
                pe.wait_ge(probs_ready, total(r, s, 1, 1))
                for t in range(T):
                    mm = pe.transpose(p_att[:, t, :], probs[:, t, :], ident[:])
                mm.then_inc(pT_psum, 1)

            def aggregate(r, s):
                pe.wait_ge(pT_ready, total(r, s, 1, 1))
                if later(r, s):
                    pe.wait_ge(hT_ready, total(r, s - 1, 2, 2))
                for t in range(T):
                    mm = pe.matmul(p_mid[t // 2][:, (t % 2) * D:(t % 2 + 1) * D],
                                   probs_T[:, t * N:(t + 1) * N], X[s % RING][:, t, :],
                                   start=True, stop=True)
                mm.then_inc(agg_ready, 1)

            def transpose_norm1(r, s):
                pe.wait_ge(norm1_ready, total(r, s, 4, 4))
                for k in range(KD):
                    for t in range(T):
                        mm = pe.transpose(p_mid[k][:, t * N:(t + 1) * N],
                                          norm1[:, t, k * P:(k + 1) * P], ident[:])
                    mm.then_inc(nT_psum, 1)

            def slot(r, s):
                if isinstance(r, int) and PER * r + s == 0:
                    pe.wait_ge(w_ready, 2 * L)
                for c in range(C):
                    if is_item(r, s):
                        hidden(r, s, c)
                    if c == 2 and is_item(r, s + 1):
                        transpose_norm1(r, s + 1)
                    if c == 3 and is_item(r, s + 2):
                        spread_sj(r, s + 2)
                    if c == 5 and is_item(r, s + 2):
                        transpose_probs(r, s + 2)
                    if c == 6 and is_item(r, s + 2):
                        aggregate(r, s + 2)
                    if c < 2 and is_item(r, s - 1):
                        feed(r, s - 1, C - 2 + c)
                    if c >= 2 and is_item(r, s):
                        feed(r, s, c - 2)

            pe.wait_ge(pool_steps, 4)
            slots(pe, slot)

        @block.scalar
        def _(act):
            def hidden(r, s, c):
                g, i, k = in_ring(s, c, G32_RING), c % GS_RING, in_ring(s, c, PF_RING)
                act.wait_ge(hid_psum, total(r, s, C, c + 1))
                if later(r, s) or c >= G32_RING:
                    act.wait_ge(g_lo_ready, total(r, s, C, c + 1 - G32_RING))
                l = layer_of(s)
                act.activation(g32[g][:], p_hid[k][:], ACT.Gelu, bias=b1_col[:, l, c:c + 1],
                               scale=1.0 / WSCALE).then_inc(gelu_ready, 1)
                act.wait_ge(gelu_ready, total(r, s, C, c + 1))
                if later(r, s) or c >= GS_RING:
                    act.wait_ge(ff_done, total(r, s, C, c + 1 - GS_RING))
                act.activation(g_hi[i][:], g32[g][:], ACT.Copy).then_inc(g_hi_ready, 1)

            def norm_apply(r, s, n, src, dst, func, done, count):
                for t in range(T):
                    act.activation(dst[:, t, :], src[:, t, :], func, bias=shift[n][:, t:t + 1],
                                   scale=rstd[n][:, t:t + 1]).then_inc(done, 1)

            def norm_input(r, s):
                act.wait_ge(rstd_ready[0], group_total(r, s, 2, 2))
                norm_apply(r, s, 0, x_in[s % 2], X[s % RING], ACT.Relu, x0_ready, 4)

            def norm_attention(r, s):
                act.wait_ge(rstd_ready[1], total(r, s, 2, 2))
                if later(r, s):
                    act.wait_ge(nT_psum, total(r, s - 1, 2, 2))
                    act.wait_ge(h_res_steps, total(r, s - 1, 2, 2))
                norm_apply(r, s, 1, res1, norm1, ACT.Identity, norm1_ready, 4)

            def norm_feed(r, s):
                act.wait_ge(rstd_ready[2], total(r, s, 2, 2))
                if later(r, s):
                    act.wait_ge(x_steps, x_total(r, s - 1, 1))
                norm_apply(r, s, 2, res2, norm2, ACT.Identity, norm2_ready, 4)

            def exponentials(r, s):
                act.wait_ge(score_steps, total(r, s, 5, 5))
                act.activation(probs[:], scores[:], ACT.Exp).then_inc(probs_ready, 1)

            def copy_probs(r, s):
                act.wait_ge(pT_psum, total(r, s, 1, 1))
                act.activation(probs_T[:], p_att[:].rearrange("p t n -> p (t n)"), ACT.Copy).then_inc(pT_ready, 1)

            def scale_hT(r, s):
                l = layer_of(s)
                if later(r, s):
                    act.wait_ge(hT_lo_ready, total(r, s - 1, 1, 1))
                for k in range(KD):
                    act.wait_ge(nT_psum, total(r, s, 2, k + 1))
                    act.activation(hT[:, k, :], p_mid[k][:], ACT.Identity, bias=beta1_col[:, l, k:k + 1],
                                   scale=g1_col[:, l, k:k + 1]).then_inc(hT_ready, 1)
                act.wait_ge(hT_ready, total(r, s, 2, 2))
                if later(r, s, 2):
                    act.wait_ge(hid_psum, total(r, s - 2, C, C))
                act.activation(hT_hi[s % 2][:], hT[:], ACT.Copy).then_inc(hT_hi_ready, 1)

            def slot(r, s):
                for c in range(C):
                    if c == 3 and is_item(r, s + 1):
                        scale_hT(r, s + 1)
                    if c == 5 and is_item(r, s + 2):
                        exponentials(r, s + 2)
                    if c == 6 and is_item(r, s + 2):
                        copy_probs(r, s + 2)
                    if is_item(r, s):
                        hidden(r, s, c)
                    if c == 1 and is_item(r, s + 1):
                        norm_attention(r, s + 1)
                    if c == 3 and is_item(r, s - 1):
                        norm_feed(r, s - 1)
                    if c == 7 and is_item(r, s + 3) and layer_of(s + 3) == 0:
                        norm_input(r, s + 3)

            act.wait_ge(const_dma, CONSTS)
            slots(act, slot)

        @block.vector
        def _(dve):
            def split_weights(l):
                for n, (w, hi, lo) in enumerate(((w1_f32, w1_hi, w1_lo), (w2_f32, w2_hi, w2_lo))):
                    dve.wait_ge(w_dma[n], 16 * (l + 1))
                    dve.tensor_scalar(hi[l][:], w[:], WSCALE, None, ALU.mult).then_inc(w_hi_ready, 1)
                    dve.wait_ge(w_hi_ready, 2 * l + n + 1)
                    dve.scalar_tensor_tensor(out=lo[l][:], in0=w[:], scalar=WSCALE, in1=hi[l][:],
                                             op0=ALU.mult, op1=ALU.subtract).then_inc(w_ready, 1)

            def hidden(r, s, c):
                g, i = in_ring(s, c, G32_RING), c % GS_RING
                dve.wait_ge(g_hi_ready, total(r, s, C, c + 1))
                dve.tensor_tensor(g_lo[i][:], g32[g][:], g_hi[i][:], ALU.subtract).then_inc(g_lo_ready, 1)

            def statistics(n, src):
                for t in range(T):
                    dve.bn_stats(bn[n][:, t, :], src[:, t, :]).then_inc(stat_steps[n], 1)

            def aggregates(n, after_8):
                for t in range(T):
                    dve.bn_aggr(mv[n][:, t, :], bn[n][:, t, :]).then_inc(stat_steps[n], 1)
                dve.wait_ge(stat_steps[n], after_8)
                dve.tensor_scalar(var_eps[n][:], mv[n][:, :, 1], EPS, None, ALU.add).then_inc(stat_steps[n], 1)
                dve.tensor_scalar(minus_mean[n][:], mv[n][:, :, 0], -1.0, None, ALU.mult).then_inc(stat_steps[n], 1)

            def input_statistics(r, s):
                dve.wait_ge(x_loaded[s % 2], lane_total(r, s))
                if later(r, s):
                    dve.wait_ge(x0_ready, group_total(r, s, 4, 0))
                statistics(0, x_in[s % 2])

            def make_mask(r, s):
                a = adj_in[s % 2]
                dve.wait_ge(pool_steps, 5)
                dve.wait_ge(adj_loaded[s % 2], lane_total(r, s))
                dve.tensor_tensor(a[:], a[:], eye_i[:].unsqueeze(1).broadcast_to([P, T, N]),
                                  ALU.add).then_inc(mask_steps, 1)
                dve.wait_ge(mask_steps, group_total(r, s, 2, 1))
                dve.tensor_scalar(mask[s % RING][:], a[:], 0.0, MASKED, ALU.is_le, ALU.mult).then_inc(mask_steps, 1)

            def dot_products(r, s):
                l, q = layer_of(s), s % RING
                if l == 0:
                    dve.wait_ge(x0_ready, group_total(r, s, 4, 4))
                else:
                    dve.wait_ge(x_steps, x_total(r, s - RING, 2))
                for t in range(T):
                    dve.tensor_tensor_reduce(out=dots[:, 2 * t, :], in0=X[q][:, t, :], in1=attn_rows[:, l, 0, :], scale=1.0,
                                             scalar=attn_b_col[:, l:l + 1], op0=ALU.mult, op1=ALU.add,
                                             accum_out=s_i[q][:, t:t + 1]).then_inc(dots_ready, 1)
                    dve.tensor_tensor_reduce(out=dots[:, 2 * t + 1, :], in0=X[q][:, t, :], in1=attn_rows[:, l, 1, :], scale=1.0,
                                             scalar=0.0, op0=ALU.mult, op1=ALU.add,
                                             accum_out=s_j[q][:, t:t + 1]).then_inc(dots_ready, 1)

            def attention_scores(r, s):
                q = s % RING
                dve.wait_ge(sj_rows_ready, total(r, s, 1, 1))
                dve.tensor_tensor(leaky[:], p_att[:], mask[q][:], ALU.add).then_inc(score_steps, 1)
                dve.wait_ge(score_steps, total(r, s, 5, 1))
                dve.wait_ge(dots_ready, total(r, s, 8, 8))
                dve.tensor_tensor(scores[:], leaky[:], s_i[q][:].unsqueeze(2).broadcast_to([P, T, N]),
                                  ALU.add).then_inc(score_steps, 1)
                dve.wait_ge(score_steps, total(r, s, 5, 2))
                dve.scalar_tensor_tensor(out=leaky[:], in0=scores[:], scalar=SLOPE, in1=scores[:],
                                         op0=ALU.mult, op1=ALU.max).then_inc(score_steps, 1)
                dve.wait_ge(score_steps, total(r, s, 5, 3))
                dve.tensor_reduce(row_max[:], leaky[:], AX.X, ALU.max).then_inc(score_steps, 1)
                dve.wait_ge(score_steps, total(r, s, 5, 4))
                dve.tensor_tensor(scores[:], leaky[:], row_max[:].unsqueeze(2).broadcast_to([P, T, N]),
                                  ALU.subtract).then_inc(score_steps, 1)

            def row_sums(r, s):
                dve.wait_ge(probs_ready, total(r, s, 1, 1))
                dve.tensor_reduce(row_sum[:], probs[:], AX.X, ALU.add).then_inc(sum_steps, 1)
                dve.wait_ge(sum_steps, total(r, s, 2, 1))
                dve.reciprocal(row_inv[:], row_sum[:]).then_inc(sum_steps, 1)

            def attention_residual(r, s):
                dve.wait_ge(agg_ready, total(r, s, 1, 1))
                dve.wait_ge(sum_steps, total(r, s, 2, 2))
                if later(r, s):
                    dve.wait_ge(norm1_ready, total(r, s - 1, 4, 4))
                for t in range(T):
                    dve.scalar_tensor_tensor(out=res1[:, t, :], in0=p_mid[t // 2][:, (t % 2) * D:(t % 2 + 1) * D],
                                             scalar=row_inv[:, t:t + 1], in1=X[s % RING][:, t, :],
                                             op0=ALU.mult, op1=ALU.add).then_inc(res1_ready, 1)
                dve.wait_ge(res1_ready, total(r, s, 4, 4))
                statistics(1, res1)

            def split_hT(r, s):
                dve.wait_ge(hT_hi_ready, total(r, s, 1, 1))
                dve.tensor_tensor(hT_lo[s % 2][:], hT[:], hT_hi[s % 2][:], ALU.subtract).then_inc(hT_lo_ready, 1)

            def feed_residual(r, s):
                dve.wait_ge(ff_done, total(r, s, C, C))
                dve.wait_ge(h_res_steps, total(r, s, 2, 2))
                if later(r, s):
                    dve.wait_ge(norm2_ready, total(r, s - 1, 4, 4))
                for b in range(2):
                    pair = slice(2 * b, 2 * b + 2)
                    dve.scalar_tensor_tensor(out=res2[:, pair, :], in0=p_ff[b][:], scalar=1.0 / WSCALE,
                                             in1=h_res[s % 2][:, pair, :],
                                             op0=ALU.mult, op1=ALU.add).then_inc(res2_ready, 1)

            def feed_statistics(r, s):
                dve.wait_ge(res2_ready, total(r, s, 2, 2))
                statistics(2, res2)

            def slot(r, s):
                starts = is_item(r, s + 3) and layer_of(s + 3) == 0
                for c in range(C):
                    if c == 1 and is_item(r, s - 1):
                        feed_residual(r, s - 1)
                    if c == 0 and is_item(r, s + 1):
                        dve.wait_ge(stat_steps[1], total(r, s + 1, 10, 4))
                    if c == 2 and is_item(r, s - 1):
                        dve.wait_ge(stat_steps[2], total(r, s - 1, 10, 4))
                    if c == 6 and starts:
                        dve.wait_ge(stat_steps[0], group_total(r, s + 3, 10, 4))
                    if is_item(r, s):
                        hidden(r, s, c)
                    if c == 0 and is_item(r, s + 1):
                        aggregates(1, total(r, s + 1, 10, 8))
                    if c == 2 and is_item(r, s - 1):
                        aggregates(2, total(r, s - 1, 10, 8))
                    if c == 6 and starts:
                        aggregates(0, group_total(r, s + 3, 10, 8))
                    if c == 0 and is_item(r, s + 2):
                        dot_products(r, s + 2)
                    if c == 1 and is_item(r, s - 1):
                        feed_statistics(r, s - 1)
                    if c == 3 and is_item(r, s + 1):
                        split_hT(r, s + 1)
                    if c == 4 and is_item(r, s + 2):
                        attention_scores(r, s + 2)
                    if c == 5 and is_item(r, s + 2):
                        row_sums(r, s + 2)
                    if c == 5 and starts:
                        input_statistics(r, s + 3)
                    if c == 6 and starts:
                        make_mask(r, s + 3)
                    if c == 7 and is_item(r, s + 2):
                        attention_residual(r, s + 2)
                if not isinstance(r, int) or r > 0:
                    return
                if s < 0:
                    split_weights(s + 3)

            dve.wait_ge(const_dma, CONSTS)
            dve.tensor_tensor(res_rows[:], res_rows[:], b2_rows[:], ALU.add).then_inc(const_steps, 1)
            slots(dve, slot)

        @block.gpsimd
        def _(pool):
            pool.memset(ident[:], 0.0).then_inc(pool_steps, 1)
            pool.memset(eye_i[:], 0).then_inc(pool_steps, 1)
            pool.memset(minus_half[:], -0.5).then_inc(pool_steps, 1)
            pool.wait_ge(pool_steps, 3)
            pool.affine_select(out=ident[:], in_=ident[:], compare_op=ALU.not_equal, fill=1.0, base=0,
                               pattern=[[-1, P]], channel_multiplier=1).then_inc(pool_steps, 1)
            pool.wait_ge(pool_steps, 4)
            pool.tensor_copy(eye_i[:], ident[:]).then_inc(pool_steps, 1)
            pool.wait_ge(const_dma, CONSTS)
            pool.wait_ge(const_steps, 1)

            def rows(v, l):
                return v[:, l, :].unsqueeze(1).broadcast_to([P, T, D])

            def inverse_deviation(n, count_stats, count_rstd):
                pool.wait_ge(stat_steps[n], count_stats)
                pool.tensor_tensor(rstd[n][:], var_eps[n][:], minus_half[:], ALU.pow).then_inc(rstd_ready[n], 1)
                pool.wait_ge(rstd_ready[n], count_rstd)
                pool.tensor_tensor(shift[n][:], minus_mean[n][:], rstd[n][:], ALU.mult).then_inc(rstd_ready[n], 1)

            def h_residual(r, s):
                l, i = layer_of(s), s % 2
                pool.wait_ge(norm1_ready, total(r, s, 4, 4))
                if later(r, s, 2):
                    pool.wait_ge(res2_ready, total(r, s - 2, 2, 2))
                pool.tensor_tensor(h_res[i][:], norm1[:], rows(g1_rows, l), ALU.mult).then_inc(h_res_steps, 1)
                pool.wait_ge(h_res_steps, total(r, s, 2, 1))
                pool.tensor_tensor(h_res[i][:], h_res[i][:], rows(res_rows, l), ALU.add).then_inc(h_res_steps, 1)

            def layer_output(r, s):
                l, q = layer_of(s), s % RING
                dst = y_out[q % 2] if l == L - 1 else X[q]
                pool.wait_ge(norm2_ready, total(r, s, 4, 4))
                if l == L - 1 and later(r, s, 2 * RING + 2):
                    pool.wait_ge(stored[q % 2], stored_total(r, q))
                pool.tensor_tensor(dst[:], norm2[:], rows(g2_rows, l), ALU.mult).then_inc(x_steps, 1)
                pool.wait_ge(x_steps, x_total(r, s, 1))
                pool.tensor_tensor(dst[:], dst[:], rows(beta2_rows, l), ALU.add).then_inc(x_steps, 1)
                if l == L - 1:
                    pool.wait_ge(x_steps, x_total(r, s, 2))
                    pool.wait_ge(x_again_loaded[q % 2], lane_total(r, s - 2 * RING))
                    pool.tensor_tensor(dst[:], dst[:], x_again[q % 2][:], ALU.add).then_inc(x_steps, 1)

            def slot(r, s):
                if is_item(r, s + 1):
                    inverse_deviation(1, total(r, s + 1, 10, 10), total(r, s + 1, 2, 1))
                    h_residual(r, s + 1)
                if is_item(r, s - 1):
                    inverse_deviation(2, total(r, s - 1, 10, 10), total(r, s - 1, 2, 1))
                    layer_output(r, s - 1)
                if is_item(r, s + 3) and layer_of(s + 3) == 0:
                    inverse_deviation(0, group_total(r, s + 3, 10, 10), group_total(r, s + 3, 2, 1))

            slots(pool, slot)

    return nc


INPUTS = ["x", "adj", "L0_gnn_attn_w", "L0_gnn_attn_b", "L0_gnn_W1", "L0_gnn_b1", "L0_gnn_W2", "L0_gnn_b2",
          "L0_gnn_g1", "L0_gnn_beta1", "L0_gnn_g2", "L0_gnn_beta2"]


def kernel(**inputs):
    import concourse.bacc as bacc
    from concourse.bass_utils import run_bass_kernel_spmd

    nc = bacc.Bacc("TRN2", target_bir_lowering=False, num_devices=1)
    arrays, args = {}, []
    for name in INPUTS:
        a = np.ascontiguousarray(inputs[name])
        arrays[f"in_{name}"] = a
        args.append(nc.dram_tensor(f"in_{name}", a.shape, mybir.dt.from_np(a.dtype), kind="ExternalInput").ap())
    out = nc.dram_tensor("out_0", (B, N, D), F32, kind="ExternalOutput").ap()
    gnn_kernel(nc, *args, out)
    return run_bass_kernel_spmd(nc, [arrays], core_ids=[0]).results[0]["out_0"]
```

```python
from contextlib import ExitStack

import numpy as np

import concourse.bass as bass
from concourse import mybir

ALU = mybir.AluOpType
ACT = mybir.ActivationFunctionType
AX = mybir.AxisListType
F32 = mybir.dt.float32
F16 = mybir.dt.float16
BF16 = mybir.dt.bfloat16
I32 = mybir.dt.int32

P = 128
B, N, D = 128, 128, 256
L = 3
H = 4 * D
T = 4
G = B // T
RING = 4
PER = RING * L
ITEMS = G * L
KD = D // P
C = H // P
TN = T * N
EPS = 1e-5
SLOPE = 0.2
MASKED = -1e30
WSCALE = 64.0
PF_RING, G32_RING, GS_RING = 3, 4, 6
LAG = 3
FIRST_SLOT = -4
FIRST_LOOP_SLOT = 4
LOOPS = ITEMS // PER - 1


def layer_of(s):
    return (s % PER) // RING


def total(r, s, per, n):
    if isinstance(r, int):
        v = per * (PER * r + s) + n
        assert v > 0
        return v
    assert per * s + n > 0
    return r * (PER * per) + (per * s + n)


def group_total(r, s, per, n):
    g = RING * (s // PER) + s % PER
    if isinstance(r, int):
        v = per * (RING * r + g) + n
        assert v > 0
        return v
    assert per * g + n > 0
    return r * (RING * per) + (per * g + n)


def lane_total(r, s):
    g = RING * (s // PER) + s % PER
    if isinstance(r, int):
        return 16 * ((RING * r + g) // 2 + 1)
    return r * (RING // 2 * 16) + 16 * (g // 2 + 1)


def x_total(r, s, n):
    v = 4 * s + RING * (s // PER) + max(0, s % PER - (PER - RING)) + n
    return (4 * PER + RING) * r + v if isinstance(r, int) else r * (4 * PER + RING) + v


def is_item(r, s):
    return not isinstance(r, int) or 0 <= PER * r + s < ITEMS


def later(r, s, m=1):
    return not isinstance(r, int) or PER * r + s - m >= 0


def in_ring(s, c, ring):
    assert PER * C % ring == 0
    return (s * C + c) % ring


def stored_total(r, q):
    return 16 * ((RING * r + q) // 2) if isinstance(r, int) else r * (8 * RING) + 16 * (q // 2)


def slots(eng, slot):
    for s in range(FIRST_SLOT, FIRST_LOOP_SLOT):
        slot(0, s)
    with eng.Fori(0, LOOPS) as r:
        for s in range(FIRST_LOOP_SLOT, FIRST_LOOP_SLOT + PER):
            slot(r, s)
    for s in range(FIRST_LOOP_SLOT, PER + 1):
        slot(LOOPS, s)


def gnn_kernel(nc, x, adj, attn_w, attn_b, W1, b1, W2, b2, g1, beta1, g2, beta2, out):
    with ExitStack() as ctx:
        def sb(name, shape, dt=F32):
            return ctx.enter_context(nc.sbuf_tensor(name, shape, dt))

        def ps(name, shape):
            return ctx.enter_context(nc.psum_tensor(name, shape, F32))

        def sem(name):
            return ctx.enter_context(nc.semaphore(name))

        ident = sb("ident", [P, P])
        eye_i = sb("eye_i", [P, N], I32)
        minus_half = sb("minus_half", [P, T])
        w1_f32 = sb("w1_f32", [P, KD, H])
        w2_f32 = sb("w2_f32", [P, C, D])
        w1_hi = [sb(f"w1_hi{l}", [P, KD, H], F16) for l in range(L)]
        w1_lo = [sb(f"w1_lo{l}", [P, KD, H], F16) for l in range(L)]
        w2_hi = [sb(f"w2_hi{l}", [P, C, D], F16) for l in range(L)]
        w2_lo = [sb(f"w2_lo{l}", [P, C, D], F16) for l in range(L)]
        b1_col = sb("b1_col", [P, L, C])
        g1_col = sb("g1_col", [P, L, KD])
        beta1_col = sb("beta1_col", [P, L, KD])
        attn_rows = sb("attn_rows", [P, L, 2, D])
        attn_b_col = sb("attn_b_col", [P, L])
        g1_rows = sb("g1_rows", [P, L, D])
        b2_rows = sb("b2_rows", [P, L, D])
        res_rows = sb("res_rows", [P, L, D])
        g2_rows = sb("g2_rows", [P, L, D])
        beta2_rows = sb("beta2_rows", [P, L, D])

        x_in = [sb(f"x_in{i}", [P, T, D]) for i in range(2)]
        adj_in = [sb(f"adj_in{i}", [P, T, N], I32) for i in range(2)]
        x_again = [sb(f"x_again{i}", [P, T, D]) for i in range(2)]
        y_out = [sb(f"y_out{i}", [P, T, D]) for i in range(2)]
        X = [sb(f"X{i}", [P, T, D]) for i in range(RING)]
        mask = [sb(f"mask{i}", [P, T, N], BF16) for i in range(RING)]

        s_i = [sb(f"s_i{i}", [P, T]) for i in range(RING)]
        s_j = [sb(f"s_j{i}", [P, T]) for i in range(RING)]
        dots = sb("dots", [P, 2 * T, D], BF16)
        scores = sb("scores", [P, T, N])
        leaky = sb("leaky", [P, T, N])
        row_max = sb("row_max", [P, T])
        probs = sb("probs", [P, T, N])
        row_sum = sb("row_sum", [P, T])
        row_inv = sb("row_inv", [P, T])
        probs_T = sb("probs_T", [P, TN])
        res1 = sb("res1", [P, T, D])
        norm1 = sb("norm1", [P, T, D])
        h_res = [sb(f"h_res{i}", [P, T, D]) for i in range(2)]
        hT = sb("hT", [P, KD, TN])
        hT_hi = [sb(f"hT_hi{i}", [P, KD, TN], F16) for i in range(2)]
        hT_lo = [sb(f"hT_lo{i}", [P, KD, TN], F16) for i in range(2)]
        g32 = [sb(f"g32_{i}", [P, TN]) for i in range(G32_RING)]
        g_hi = [sb(f"g_hi{i}", [P, TN], F16) for i in range(GS_RING)]
        g_lo = [sb(f"g_lo{i}", [P, TN], F16) for i in range(GS_RING)]
        res2 = sb("res2", [P, T, D])
        norm2 = sb("norm2", [P, T, D])
        bn = [sb(f"bn{i}", [P, T, 6]) for i in range(3)]
        mv = [sb(f"mv{i}", [P, T, 2]) for i in range(3)]
        var_eps = [sb(f"var_eps{i}", [P, T]) for i in range(3)]
        minus_mean = [sb(f"minus_mean{i}", [P, T]) for i in range(3)]
        rstd = [sb(f"rstd{i}", [P, T]) for i in range(3)]
        shift = [sb(f"shift{i}", [P, T]) for i in range(3)]

        p_hid = [ps(f"p_hid{i}", [P, TN]) for i in range(PF_RING)]
        p_att = ps("p_att", [P, T, N])
        p_pair = [[ps(f"p_pair{i}{b}", [P, T // 2, D]) for b in range(2)] for i in range(2)]

        def ff_banks(s):
            return p_pair[s % 2]

        def nT_banks(s):
            return [p[:].rearrange("p t d -> p (t d)") for p in p_pair[s % 2]]

        def agg_banks(s):
            return p_pair[(s - 1) % 2]

        const_dma = sem("const_dma")
        w_dma = [sem("w1_dma"), sem("w2_dma")]
        const_steps = sem("const_steps")
        pool_steps = sem("pool_steps")
        w_hi_ready, w_ready = sem("w_hi_ready"), sem("w_ready")
        x_loaded = [sem(f"x_loaded{i}") for i in range(2)]
        adj_loaded = [sem(f"adj_loaded{i}") for i in range(2)]
        x_again_loaded = [sem(f"x_again_loaded{i}") for i in range(2)]
        stored = [sem(f"stored{i}") for i in range(2)]
        mask_steps = sem("mask_steps")
        x0_ready = sem("x0_ready")
        dots_ready = sem("dots_ready")
        sj_rows_ready = sem("sj_rows_ready")
        score_steps = sem("score_steps")
        probs_ready = sem("probs_ready")
        sum_steps = sem("sum_steps")
        pT_psum = sem("pT_psum")
        pT_ready = sem("pT_ready")
        agg_ready = sem("agg_ready")
        res1_ready = sem("res1_ready")
        stat_steps = [sem(f"stat_steps{i}") for i in range(3)]
        rstd_ready = [sem(f"rstd_ready{i}") for i in range(3)]
        norm1_ready = sem("norm1_ready")
        nT_psum = sem("nT_psum")
        hT_ready = sem("hT_ready")
        hT_hi_ready = sem("hT_hi_ready")
        hT_lo_ready = sem("hT_lo_ready")
        h_res_steps = sem("h_res_steps")
        hid_psum = sem("hid_psum")
        gelu_ready = sem("gelu_ready")
        g_hi_ready = sem("g_hi_ready")
        g_lo_ready = sem("g_lo_ready")
        ff_done = sem("ff_done")
        res2_ready = sem("res2_ready")
        norm2_ready = sem("norm2_ready")
        x_steps = sem("x_steps")

        block = ctx.enter_context(nc.Block())
        CONSTS = 10 * 16

        @block.sync
        def _(sp):
            with nc.allow_non_contiguous_dma("columns of small vectors"):
                for dst, src in (
                    (b1_col[:], b1.rearrange("l (c p) -> p l c", p=P)),
                    (g1_col[:], g1.rearrange("l (c p) -> p l c", p=P)),
                    (beta1_col[:], beta1.rearrange("l (c p) -> p l c", p=P)),
                ):
                    sp.dma_start(dst, src).then_inc(const_dma, 16)
            for dst, src in (
                (attn_rows[:].rearrange("p l a d -> p (l a d)"), attn_w.rearrange("l e -> (l e)")),
                (attn_b_col[:], attn_b),
                (g1_rows[:].rearrange("p l d -> p (l d)"), g1.rearrange("l d -> (l d)")),
                (b2_rows[:].rearrange("p l d -> p (l d)"), b2.rearrange("l d -> (l d)")),
                (res_rows[:].rearrange("p l d -> p (l d)"), beta1.rearrange("l d -> (l d)")),
                (g2_rows[:].rearrange("p l d -> p (l d)"), g2.rearrange("l d -> (l d)")),
                (beta2_rows[:].rearrange("p l d -> p (l d)"), beta2.rearrange("l d -> (l d)")),
            ):
                sp.dma_start(dst, src.partition_broadcast(P)).then_inc(const_dma, 16)

            def weights(l):
                if l >= 1:
                    sp.wait_ge(w_ready, 2 * l - 1)
                sp.dma_start(w1_f32[:], W1[l].rearrange("(k p) h -> p k h", p=P)).then_inc(w_dma[0], 16)
                if l >= 1:
                    sp.wait_ge(w_ready, 2 * l)
                sp.dma_start(w2_f32[:], W2[l].rearrange("(c p) d -> p c d", p=P)).then_inc(w_dma[1], 16)

            def graphs(tensor, g):
                v = tensor.rearrange("(g t) n d -> n g t d", t=T)
                if isinstance(g, int):
                    return v[:, g]
                return v[:, bass.ds(g, 1)].rearrange("n g t d -> n (g t) d")

            def load_x(g, i):
                sp.dma_start(x_in[i][:], graphs(x, g)).then_inc(x_loaded[i], 16)

            def load_adj(g, i):
                sp.dma_start(adj_in[i][:], graphs(adj, g)).then_inc(adj_loaded[i], 16)

            def load_again(g, i):
                sp.dma_start(x_again[i][:], graphs(x, g)).then_inc(x_again_loaded[i], 16)

            def store(g, i):
                sp.dma_start(graphs(out, g), y_out[i][:]).then_inc(stored[i], 16)

            for g in range(2):
                load_x(g, g)
                load_adj(g, g)
            weights(0)
            for g in (2, 3, 4):
                sp.wait_ge(x0_ready, 4 * (g - 1))
                load_x(g, g % 2)
                sp.wait_ge(mask_steps, 2 * (g - 1))
                load_adj(g, g % 2)
                if g <= L:
                    weights(g - 1)
            load_again(0, 0)
            load_again(1, 1)
            with sp.Fori(0, LOOPS - 1) as r:
                for q in range(RING):
                    i, g = q % 2, r * RING + q
                    sp.wait_ge(x0_ready, r * (4 * RING) + 4 * (RING + q))
                    load_x(g + (RING + 1), 1 - i)
                    sp.wait_ge(mask_steps, r * (2 * RING) + 2 * (RING + q))
                    load_adj(g + (RING + 1), 1 - i)
                    sp.wait_ge(x_steps, x_total(r, 2 * RING + q, 5))
                    store(g, i)
                    load_again(g + 2, i)
            for g in range(RING * (LOOPS - 1), G):
                if g + RING + 1 < G:
                    sp.wait_ge(x0_ready, 4 * (g + RING))
                    load_x(g + RING + 1, (g + 1) % 2)
                    sp.wait_ge(mask_steps, 2 * (g + RING))
                    load_adj(g + RING + 1, (g + 1) % 2)
                sp.wait_ge(x_steps, x_total(g // RING, 2 * RING + g % RING, 5))
                store(g, g % 2)
                if g + 2 < G:
                    load_again(g + 2, g % 2)
            for i in range(2):
                sp.wait_ge(stored[i], 16 * G // 2)

        @block.tensor
        def _(pe):
            def hidden(r, s, c):
                l, i = layer_of(s), s % 2
                if c == 0:
                    pe.wait_ge(hT_hi_ready, total(r, s, 1, 1))
                    pe.wait_ge(hT_lo_ready, total(r, s, 1, 1))
                if later(r, s) or c >= PF_RING:
                    pe.wait_ge(gelu_ready, total(r, s, C, c + 1 - PF_RING))
                cols = slice(c * P, (c + 1) * P)
                for n, (k, w, h) in enumerate((k, w, h) for k in range(KD) for w, h in
                                              ((w1_hi, hT_hi), (w1_hi, hT_lo), (w1_lo, hT_hi))):
                    mm = pe.matmul(p_hid[in_ring(s, c, PF_RING)][:], w[l][:, k, cols], h[i][:, k, :],
                                   start=(n == 0), stop=(n == 3 * KD - 1))
                mm.then_inc(hid_psum, 1)

            def feed(r, s, c):
                l, i = layer_of(s), in_ring(s, c, GS_RING)
                if c == 0 and is_item(r, s + 1):
                    pe.wait_ge(res1_ready, total(r, s + 1, 4, 4))
                pe.wait_ge(g_hi_ready, total(r, s, C, c + 1))
                pe.wait_ge(g_lo_ready, total(r, s, C, c + 1))
                for t in range(T):
                    nodes = slice(t * N, (t + 1) * N)
                    for n, (g, w) in enumerate(((g_hi, w2_hi), (g_hi, w2_lo), (g_lo, w2_hi))):
                        mm = pe.matmul(ff_banks(s)[t // 2][:, t % 2, :], g[i][:, nodes], w[l][:, c, :],
                                       start=(c == 0 and t % 2 == 0 and n == 0),
                                       stop=(c == C - 1 and n == 2), skip_group_check=True)
                mm.then_inc(ff_done, 1)

            def spread_sj(r, s):
                pe.wait_ge(dots_ready, total(r, s, 8, 8))
                if later(r, s):
                    pe.wait_ge(pT_ready, total(r, s - 1, 1, 1))
                for t in range(T):
                    mm = pe.transpose(p_att[:, t, :], s_j[s % RING][:, t:t + 1].broadcast_to([P, P]), ident[:])
                mm.then_inc(sj_rows_ready, 1)

            def transpose_probs(r, s):
                pe.wait_ge(probs_ready, total(r, s, 1, 1))
                for t in range(T):
                    mm = pe.transpose(p_att[:, t, :], probs[:, t, :], ident[:])
                mm.then_inc(pT_psum, 1)

            def aggregate(r, s):
                pe.wait_ge(pT_ready, total(r, s, 1, 1))
                if later(r, s):
                    pe.wait_ge(hT_ready, total(r, s - 1, 2, 2))
                for t in range(T):
                    mm = pe.matmul(agg_banks(s)[t // 2][:, t % 2, :],
                                   probs_T[:, t * N:(t + 1) * N], X[s % RING][:, t, :],
                                   start=True, stop=True)
                mm.then_inc(agg_ready, 1)

            def transpose_norm1(r, s):
                if later(r, s, 2):
                    pe.wait_ge(res2_ready, total(r, s - 2, 2, 2))
                pe.wait_ge(norm1_ready, total(r, s, 4, 4))
                for k in range(KD):
                    for t in range(T):
                        mm = pe.transpose(nT_banks(s)[k][:, t * N:(t + 1) * N],
                                          norm1[:, t, k * P:(k + 1) * P], ident[:])
                    mm.then_inc(nT_psum, 1)

            def slot(r, s):
                if isinstance(r, int) and PER * r + s == 0:
                    pe.wait_ge(w_ready, 2 * L)
                for c in range(C):
                    if is_item(r, s):
                        hidden(r, s, c)
                    if c == 3 and is_item(r, s + 2):
                        spread_sj(r, s + 2)
                    if c == 4 and is_item(r, s + 1):
                        transpose_norm1(r, s + 1)
                    if c < LAG and is_item(r, s - 1):
                        feed(r, s - 1, C - LAG + c)
                    if c >= LAG and is_item(r, s):
                        feed(r, s, c - LAG)
                    if c == 6 and is_item(r, s + 2):
                        transpose_probs(r, s + 2)
                    if c == 7 and is_item(r, s + 2):
                        aggregate(r, s + 2)

            pe.wait_ge(pool_steps, 4)
            slots(pe, slot)

        @block.scalar
        def _(act):
            def hidden(r, s, c):
                g, i, k = (in_ring(s, c, n) for n in (G32_RING, GS_RING, PF_RING))
                act.wait_ge(hid_psum, total(r, s, C, c + 1))
                if later(r, s) or c >= G32_RING:
                    act.wait_ge(g_lo_ready, total(r, s, C, c + 1 - G32_RING))
                l = layer_of(s)
                act.activation(g32[g][:], p_hid[k][:], ACT.Gelu, bias=b1_col[:, l, c:c + 1],
                               scale=1.0 / WSCALE).then_inc(gelu_ready, 1)
                act.wait_ge(gelu_ready, total(r, s, C, c + 1))
                if later(r, s) or c >= GS_RING:
                    act.wait_ge(ff_done, total(r, s, C, c + 1 - GS_RING))
                act.activation(g_hi[i][:], g32[g][:], ACT.Copy).then_inc(g_hi_ready, 1)

            def norm_apply(r, s, n, src, dst, func, done, count):
                for t in range(T):
                    act.activation(dst[:, t, :], src[:, t, :], func, bias=shift[n][:, t:t + 1],
                                   scale=rstd[n][:, t:t + 1]).then_inc(done, 1)

            def norm_input(r, s):
                act.wait_ge(rstd_ready[0], group_total(r, s, 2, 2))
                norm_apply(r, s, 0, x_in[s % 2], X[s % RING], ACT.Relu, x0_ready, 4)

            def norm_attention(r, s):
                act.wait_ge(rstd_ready[1], total(r, s, 2, 2))
                if later(r, s):
                    act.wait_ge(nT_psum, total(r, s - 1, 2, 2))
                    act.wait_ge(h_res_steps, total(r, s - 1, 2, 2))
                norm_apply(r, s, 1, res1, norm1, ACT.Identity, norm1_ready, 4)

            def norm_feed(r, s):
                act.wait_ge(rstd_ready[2], total(r, s, 2, 2))
                if later(r, s):
                    act.wait_ge(x_steps, x_total(r, s - 1, 3))
                norm_apply(r, s, 2, res2, norm2, ACT.Identity, norm2_ready, 4)

            def exponentials(r, s):
                act.wait_ge(score_steps, total(r, s, 5, 5))
                act.activation(probs[:], scores[:], ACT.Exp).then_inc(probs_ready, 1)

            def copy_probs(r, s):
                act.wait_ge(pT_psum, total(r, s, 1, 1))
                act.activation(probs_T[:], p_att[:].rearrange("p t n -> p (t n)"), ACT.Copy).then_inc(pT_ready, 1)

            def scale_hT(r, s):
                l = layer_of(s)
                if later(r, s):
                    act.wait_ge(hT_lo_ready, total(r, s - 1, 1, 1))
                for k in range(KD):
                    act.wait_ge(nT_psum, total(r, s, 2, k + 1))
                    act.activation(hT[:, k, :], nT_banks(s)[k], ACT.Identity, bias=beta1_col[:, l, k:k + 1],
                                   scale=g1_col[:, l, k:k + 1]).then_inc(hT_ready, 1)
                act.wait_ge(hT_ready, total(r, s, 2, 2))
                if later(r, s, 2):
                    act.wait_ge(hid_psum, total(r, s - 2, C, C))
                act.activation(hT_hi[s % 2][:], hT[:], ACT.Copy).then_inc(hT_hi_ready, 1)

            def slot(r, s):
                for c in range(C):
                    if is_item(r, s):
                        hidden(r, s, c)
                    if c == 1 and is_item(r, s + 3) and layer_of(s + 3) == 0:
                        norm_input(r, s + 3)
                    if c == 2 and is_item(r, s + 1):
                        norm_attention(r, s + 1)
                    if c == 4 and is_item(r, s + 1):
                        scale_hT(r, s + 1)
                    if c == 5 and is_item(r, s + 2):
                        exponentials(r, s + 2)
                    if c == 6 and is_item(r, s + 2):
                        copy_probs(r, s + 2)
                    if c == 6 and is_item(r, s - 1):
                        norm_feed(r, s - 1)

            act.wait_ge(const_dma, CONSTS)
            slots(act, slot)

        @block.vector
        def _(dve):
            def split_weights(l):
                for n, (w, hi, lo) in enumerate(((w1_f32, w1_hi, w1_lo), (w2_f32, w2_hi, w2_lo))):
                    dve.wait_ge(w_dma[n], 16 * (l + 1))
                    dve.tensor_scalar(hi[l][:], w[:], WSCALE, None, ALU.mult).then_inc(w_hi_ready, 1)
                    dve.wait_ge(w_hi_ready, 2 * l + n + 1)
                    dve.scalar_tensor_tensor(out=lo[l][:], in0=w[:], scalar=WSCALE, in1=hi[l][:],
                                             op0=ALU.mult, op1=ALU.subtract).then_inc(w_ready, 1)

            def hidden(r, s, c):
                g, i = in_ring(s, c, G32_RING), in_ring(s, c, GS_RING)
                dve.wait_ge(g_hi_ready, total(r, s, C, c + 1))
                dve.tensor_tensor(g_lo[i][:], g32[g][:], g_hi[i][:], ALU.subtract).then_inc(g_lo_ready, 1)

            def statistics(n, src):
                for t in range(T):
                    dve.bn_stats(bn[n][:, t, :], src[:, t, :]).then_inc(stat_steps[n], 1)

            def aggregates(n, after_8):
                for t in range(T):
                    dve.bn_aggr(mv[n][:, t, :], bn[n][:, t, :]).then_inc(stat_steps[n], 1)
                dve.wait_ge(stat_steps[n], after_8)
                dve.tensor_scalar(var_eps[n][:], mv[n][:, :, 1], EPS, None, ALU.add).then_inc(stat_steps[n], 1)
                dve.tensor_scalar(minus_mean[n][:], mv[n][:, :, 0], -1.0, None, ALU.mult).then_inc(stat_steps[n], 1)

            def input_statistics(r, s):
                dve.wait_ge(x_loaded[s % 2], lane_total(r, s))
                if later(r, s):
                    dve.wait_ge(x0_ready, group_total(r, s, 4, 0))
                statistics(0, x_in[s % 2])

            def make_mask(r, s):
                a = adj_in[s % 2]
                dve.wait_ge(pool_steps, 5)
                dve.wait_ge(adj_loaded[s % 2], lane_total(r, s))
                dve.tensor_tensor(a[:], a[:], eye_i[:].unsqueeze(1).broadcast_to([P, T, N]),
                                  ALU.add).then_inc(mask_steps, 1)
                dve.wait_ge(mask_steps, group_total(r, s, 2, 1))
                dve.tensor_scalar(mask[s % RING][:], a[:], 0.0, MASKED, ALU.is_le, ALU.mult).then_inc(mask_steps, 1)

            def dot_products(r, s, pair):
                l, q = layer_of(s), s % RING
                if l == 0:
                    dve.wait_ge(x0_ready, group_total(r, s, 4, 2 * pair + 2))
                else:
                    dve.wait_ge(x_steps, x_total(r, s - RING, 2 * pair + 2))
                for t in (2 * pair, 2 * pair + 1):
                    dve.tensor_tensor_reduce(out=dots[:, 2 * t, :], in0=X[q][:, t, :], in1=attn_rows[:, l, 0, :], scale=1.0,
                                             scalar=attn_b_col[:, l:l + 1], op0=ALU.mult, op1=ALU.add,
                                             accum_out=s_i[q][:, t:t + 1]).then_inc(dots_ready, 1)
                    dve.tensor_tensor_reduce(out=dots[:, 2 * t + 1, :], in0=X[q][:, t, :], in1=attn_rows[:, l, 1, :], scale=1.0,
                                             scalar=0.0, op0=ALU.mult, op1=ALU.add,
                                             accum_out=s_j[q][:, t:t + 1]).then_inc(dots_ready, 1)

            def add_scores(r, s):
                q = s % RING
                dve.wait_ge(sj_rows_ready, total(r, s, 1, 1))
                dve.tensor_tensor(leaky[:], p_att[:], mask[q][:], ALU.add).then_inc(score_steps, 1)
                dve.wait_ge(score_steps, total(r, s, 5, 1))
                dve.wait_ge(dots_ready, total(r, s, 8, 8))
                dve.tensor_tensor(scores[:], leaky[:], s_i[q][:].unsqueeze(2).broadcast_to([P, T, N]),
                                  ALU.add).then_inc(score_steps, 1)

            def leaky_scores(r, s):
                dve.wait_ge(score_steps, total(r, s, 5, 2))
                dve.scalar_tensor_tensor(out=leaky[:], in0=scores[:], scalar=SLOPE, in1=scores[:],
                                         op0=ALU.mult, op1=ALU.max).then_inc(score_steps, 1)

            def shift_scores(r, s):
                dve.wait_ge(score_steps, total(r, s, 5, 3))
                dve.tensor_reduce(row_max[:], leaky[:], AX.X, ALU.max).then_inc(score_steps, 1)
                dve.wait_ge(score_steps, total(r, s, 5, 4))
                dve.tensor_tensor(scores[:], leaky[:], row_max[:].unsqueeze(2).broadcast_to([P, T, N]),
                                  ALU.subtract).then_inc(score_steps, 1)

            def row_sums(r, s):
                dve.wait_ge(probs_ready, total(r, s, 1, 1))
                dve.tensor_reduce(row_sum[:], probs[:], AX.X, ALU.add).then_inc(sum_steps, 1)
                dve.wait_ge(sum_steps, total(r, s, 2, 1))
                dve.reciprocal(row_inv[:], row_sum[:]).then_inc(sum_steps, 1)

            def attention_residual(r, s):
                dve.wait_ge(agg_ready, total(r, s, 1, 1))
                dve.wait_ge(sum_steps, total(r, s, 2, 2))
                if later(r, s):
                    dve.wait_ge(norm1_ready, total(r, s - 1, 4, 4))
                for t in range(T):
                    dve.scalar_tensor_tensor(out=res1[:, t, :], in0=agg_banks(s)[t // 2][:, t % 2, :],
                                             scalar=row_inv[:, t:t + 1], in1=X[s % RING][:, t, :],
                                             op0=ALU.mult, op1=ALU.add).then_inc(res1_ready, 1)

            def attention_statistics(r, s):
                dve.wait_ge(res1_ready, total(r, s, 4, 4))
                statistics(1, res1)

            def split_hT(r, s):
                dve.wait_ge(hT_hi_ready, total(r, s, 1, 1))
                dve.tensor_tensor(hT_lo[s % 2][:], hT[:], hT_hi[s % 2][:], ALU.subtract).then_inc(hT_lo_ready, 1)

            def feed_residual(r, s):
                dve.wait_ge(ff_done, total(r, s, C, C))
                dve.wait_ge(h_res_steps, total(r, s, 2, 2))
                if later(r, s):
                    dve.wait_ge(norm2_ready, total(r, s - 1, 4, 4))
                for b in range(2):
                    pair = slice(2 * b, 2 * b + 2)
                    dve.scalar_tensor_tensor(out=res2[:, pair, :], in0=ff_banks(s)[b][:], scalar=1.0 / WSCALE,
                                             in1=h_res[s % 2][:, pair, :],
                                             op0=ALU.mult, op1=ALU.add).then_inc(res2_ready, 1)

            def feed_statistics(r, s):
                dve.wait_ge(res2_ready, total(r, s, 2, 2))
                statistics(2, res2)

            def slot(r, s):
                starts = is_item(r, s + 4) and layer_of(s + 4) == 0
                for c in range(C):
                    if c == 3 and is_item(r, s - 1):
                        feed_residual(r, s - 1)
                    if c == 1 and is_item(r, s + 1):
                        dve.wait_ge(stat_steps[1], total(r, s + 1, 10, 4))
                    if c == 5 and is_item(r, s - 1):
                        dve.wait_ge(stat_steps[2], total(r, s - 1, 10, 4))
                    if c == 7 and starts:
                        dve.wait_ge(stat_steps[0], group_total(r, s + 4, 10, 4))
                    if is_item(r, s):
                        hidden(r, s, c)
                    if c == 0 and is_item(r, s + 1):
                        attention_statistics(r, s + 1)
                    if c == 1 and is_item(r, s + 1):
                        aggregates(1, total(r, s + 1, 10, 8))
                    if c in (0, 1) and is_item(r, s + 2):
                        dot_products(r, s + 2, c)
                    if c == 2 and is_item(r, s + 2):
                        add_scores(r, s + 2)
                    if c == 3 and is_item(r, s + 2):
                        leaky_scores(r, s + 2)
                    if c == 4 and is_item(r, s + 2):
                        shift_scores(r, s + 2)
                    if c == 4 and is_item(r, s - 1):
                        feed_statistics(r, s - 1)
                    if c == 5 and is_item(r, s - 1):
                        aggregates(2, total(r, s - 1, 10, 8))
                    if c == 6 and is_item(r, s + 1):
                        split_hT(r, s + 1)
                    if c == 6 and is_item(r, s + 2):
                        row_sums(r, s + 2)
                    if c == 6 and starts:
                        input_statistics(r, s + 4)
                    if c == 7 and is_item(r, s + 2):
                        attention_residual(r, s + 2)
                    if c == 7 and starts:
                        aggregates(0, group_total(r, s + 4, 10, 8))
                        make_mask(r, s + 4)
                if not isinstance(r, int) or r > 0:
                    return
                if s < -1:
                    split_weights(s + 4)

            dve.wait_ge(const_dma, CONSTS)
            dve.tensor_tensor(res_rows[:], res_rows[:], b2_rows[:], ALU.add).then_inc(const_steps, 1)
            slots(dve, slot)

        @block.gpsimd
        def _(pool):
            pool.memset(ident[:], 0.0).then_inc(pool_steps, 1)
            pool.memset(eye_i[:], 0).then_inc(pool_steps, 1)
            pool.memset(minus_half[:], -0.5).then_inc(pool_steps, 1)
            pool.wait_ge(pool_steps, 3)
            pool.affine_select(out=ident[:], in_=ident[:], compare_op=ALU.not_equal, fill=1.0, base=0,
                               pattern=[[-1, P]], channel_multiplier=1).then_inc(pool_steps, 1)
            pool.wait_ge(pool_steps, 4)
            pool.tensor_copy(eye_i[:], ident[:]).then_inc(pool_steps, 1)
            pool.wait_ge(const_dma, CONSTS)
            pool.wait_ge(const_steps, 1)

            def rows(v, l, graphs=2):
                return v[:, l, :].unsqueeze(1).broadcast_to([P, graphs, D])

            def inverse_deviation(n, count_stats, count_rstd):
                pool.wait_ge(stat_steps[n], count_stats)
                pool.tensor_tensor(rstd[n][:], var_eps[n][:], minus_half[:], ALU.pow).then_inc(rstd_ready[n], 1)
                pool.wait_ge(rstd_ready[n], count_rstd)
                pool.tensor_tensor(shift[n][:], minus_mean[n][:], rstd[n][:], ALU.mult).then_inc(rstd_ready[n], 1)

            def h_residual(r, s):
                l, i = layer_of(s), s % 2
                pool.wait_ge(norm1_ready, total(r, s, 4, 4))
                if later(r, s, 2):
                    pool.wait_ge(res2_ready, total(r, s - 2, 2, 2))
                pool.tensor_tensor(h_res[i][:], norm1[:], rows(g1_rows, l, T), ALU.mult).then_inc(h_res_steps, 1)
                pool.wait_ge(h_res_steps, total(r, s, 2, 1))
                pool.tensor_tensor(h_res[i][:], h_res[i][:], rows(res_rows, l, T), ALU.add).then_inc(h_res_steps, 1)

            def layer_output(r, s):
                l, q = layer_of(s), s % RING
                dst = y_out[q % 2] if l == L - 1 else X[q]
                if l == L - 1 and later(r, s, 2 * RING + 2):
                    pool.wait_ge(stored[q % 2], stored_total(r, q))
                for p in range(2):
                    pair = slice(2 * p, 2 * p + 2)
                    pool.wait_ge(norm2_ready, total(r, s, 4, 2 * p + 2))
                    pool.tensor_tensor(dst[:, pair, :], norm2[:, pair, :], rows(g2_rows, l), ALU.mult).then_inc(x_steps, 1)
                    pool.wait_ge(x_steps, x_total(r, s, 2 * p + 1))
                    pool.tensor_tensor(dst[:, pair, :], dst[:, pair, :], rows(beta2_rows, l), ALU.add).then_inc(x_steps, 1)
                if l == L - 1:
                    pool.wait_ge(x_steps, x_total(r, s, 4))
                    pool.wait_ge(x_again_loaded[q % 2], lane_total(r, s - 2 * RING))
                    pool.tensor_tensor(dst[:], dst[:], x_again[q % 2][:], ALU.add).then_inc(x_steps, 1)

            def slot(r, s):
                if is_item(r, s + 1):
                    inverse_deviation(1, total(r, s + 1, 10, 10), total(r, s + 1, 2, 1))
                    h_residual(r, s + 1)
                if is_item(r, s - 1):
                    inverse_deviation(2, total(r, s - 1, 10, 10), total(r, s - 1, 2, 1))
                    layer_output(r, s - 1)
                if is_item(r, s + 4) and layer_of(s + 4) == 0:
                    inverse_deviation(0, group_total(r, s + 4, 10, 10), group_total(r, s + 4, 2, 1))

            slots(pool, slot)

    return nc


INPUTS = ["x", "adj", "L0_gnn_attn_w", "L0_gnn_attn_b", "L0_gnn_W1", "L0_gnn_b1", "L0_gnn_W2", "L0_gnn_b2",
          "L0_gnn_g1", "L0_gnn_beta1", "L0_gnn_g2", "L0_gnn_beta2"]


def kernel(**inputs):
    import concourse.bacc as bacc
    from concourse.bass_utils import run_bass_kernel_spmd

    nc = bacc.Bacc("TRN2", target_bir_lowering=False, num_devices=1)
    arrays, args = {}, []
    for name in INPUTS:
        a = np.ascontiguousarray(inputs[name])
        arrays[f"in_{name}"] = a
        args.append(nc.dram_tensor(f"in_{name}", a.shape, mybir.dt.from_np(a.dtype), kind="ExternalInput").ap())
    out = nc.dram_tensor("out_0", (B, N, D), F32, kind="ExternalOutput").ap()
    gnn_kernel(nc, *args, out)
    return run_bass_kernel_spmd(nc, [arrays], core_ids=[0]).results[0]["out_0"]
```

```python
from contextlib import ExitStack

import numpy as np

import concourse.bass as bass
from concourse import mybir

ALU = mybir.AluOpType
ACT = mybir.ActivationFunctionType
AX = mybir.AxisListType
F32 = mybir.dt.float32
F16 = mybir.dt.float16
BF16 = mybir.dt.bfloat16
I32 = mybir.dt.int32

P = 128
B, N, D = 128, 128, 256
L = 3
H = 4 * D
T = 4
G = B // T
RING = 4
PER = RING * L
ITEMS = G * L
KD = D // P
C = H // P
TN = T * N
EPS = 1e-5
SLOPE = 0.2
MASKED = -1e30
WSCALE = 64.0
PF_RING, G32_RING, GS_RING = 3, 4, 6
LAG = 3
FIRST_SLOT = -4
FIRST_LOOP_SLOT = 4
LOOPS = ITEMS // PER - 1


def layer_of(s):
    return (s % PER) // RING


def total(r, s, per, n):
    if isinstance(r, int):
        v = per * (PER * r + s) + n
        assert v > 0
        return v
    assert per * s + n > 0
    return r * (PER * per) + (per * s + n)


def group_total(r, s, per, n):
    g = RING * (s // PER) + s % PER
    if isinstance(r, int):
        v = per * (RING * r + g) + n
        assert v > 0
        return v
    assert per * g + n > 0
    return r * (RING * per) + (per * g + n)


def lane_total(r, s):
    g = RING * (s // PER) + s % PER
    if isinstance(r, int):
        return 16 * ((RING * r + g) // 2 + 1)
    return r * (RING // 2 * 16) + 16 * (g // 2 + 1)


def x_total(r, s, n):
    v = 4 * s + RING * (s // PER) + max(0, s % PER - (PER - RING)) + n
    return (4 * PER + RING) * r + v if isinstance(r, int) else r * (4 * PER + RING) + v


def is_item(r, s):
    return not isinstance(r, int) or 0 <= PER * r + s < ITEMS


def later(r, s, m=1):
    return not isinstance(r, int) or PER * r + s - m >= 0


def in_ring(s, c, ring):
    assert PER * C % ring == 0
    return (s * C + c) % ring


def stored_total(r, q):
    return 16 * ((RING * r + q) // 2) if isinstance(r, int) else r * (8 * RING) + 16 * (q // 2)


def slots(eng, slot):
    for s in range(FIRST_SLOT, FIRST_LOOP_SLOT):
        slot(0, s)
    with eng.Fori(0, LOOPS) as r:
        for s in range(FIRST_LOOP_SLOT, FIRST_LOOP_SLOT + PER):
            slot(r, s)
    for s in range(FIRST_LOOP_SLOT, PER + 1):
        slot(LOOPS, s)


def gnn_kernel(nc, x, adj, attn_w, attn_b, W1, b1, W2, b2, g1, beta1, g2, beta2, out):
    with ExitStack() as ctx:
        def sb(name, shape, dt=F32):
            return ctx.enter_context(nc.sbuf_tensor(name, shape, dt))

        def ps(name, shape):
            return ctx.enter_context(nc.psum_tensor(name, shape, F32))

        def sem(name):
            return ctx.enter_context(nc.semaphore(name))

        ident = sb("ident", [P, P])
        eye_i = sb("eye_i", [P, N], I32)
        minus_half = sb("minus_half", [P, T])
        w1_f32 = sb("w1_f32", [P, KD, H])
        w2_f32 = sb("w2_f32", [P, C, D])
        w1_hi = [sb(f"w1_hi{l}", [P, KD, H], F16) for l in range(L)]
        w1_lo = [sb(f"w1_lo{l}", [P, KD, H], F16) for l in range(L)]
        w2_hi = [sb(f"w2_hi{l}", [P, C, D], F16) for l in range(L)]
        w2_lo = [sb(f"w2_lo{l}", [P, C, D], F16) for l in range(L)]
        b1_col = sb("b1_col", [P, L, C])
        g1_col = sb("g1_col", [P, L, KD])
        beta1_col = sb("beta1_col", [P, L, KD])
        attn_rows = sb("attn_rows", [P, L, 2, D])
        attn_b_col = sb("attn_b_col", [P, L])
        g1_rows = sb("g1_rows", [P, L, D])
        b2_rows = sb("b2_rows", [P, L, D])
        res_rows = sb("res_rows", [P, L, D])
        g2_rows = sb("g2_rows", [P, L, D])
        beta2_rows = sb("beta2_rows", [P, L, D])

        x_in = [sb(f"x_in{i}", [P, T, D]) for i in range(2)]
        adj_in = [sb(f"adj_in{i}", [P, T, N], I32) for i in range(2)]
        x_again = [sb(f"x_again{i}", [P, T, D]) for i in range(2)]
        y_out = [sb(f"y_out{i}", [P, T, D]) for i in range(2)]
        X = [sb(f"X{i}", [P, T, D]) for i in range(RING)]
        mask = [sb(f"mask{i}", [P, T, N], BF16) for i in range(RING)]

        s_i = [sb(f"s_i{i}", [P, T]) for i in range(RING)]
        s_j = [sb(f"s_j{i}", [P, T]) for i in range(RING)]
        dots = sb("dots", [P, 2 * T, D], BF16)
        scores = sb("scores", [P, T, N])
        leaky = sb("leaky", [P, T, N])
        row_max = sb("row_max", [P, T])
        probs = sb("probs", [P, T, N])
        row_sum = sb("row_sum", [P, T])
        row_inv = sb("row_inv", [P, T])
        pT_hi, pT_lo = sb("pT_hi", [P, TN], F16), sb("pT_lo", [P, TN], F16)
        X_hi, X_lo = sb("X_hi", [P, T, D], F16), sb("X_lo", [P, T, D], F16)
        res1 = sb("res1", [P, T, D])
        norm1 = sb("norm1", [P, T, D])
        h_res = [sb(f"h_res{i}", [P, T, D]) for i in range(2)]
        hT = sb("hT", [P, KD, TN])
        hT_hi = [sb(f"hT_hi{i}", [P, KD, TN], F16) for i in range(2)]
        hT_lo = [sb(f"hT_lo{i}", [P, KD, TN], F16) for i in range(2)]
        g32 = [sb(f"g32_{i}", [P, TN]) for i in range(G32_RING)]
        g_hi = [sb(f"g_hi{i}", [P, TN], F16) for i in range(GS_RING)]
        g_lo = [sb(f"g_lo{i}", [P, TN], F16) for i in range(GS_RING)]
        res2 = sb("res2", [P, T, D])
        norm2 = sb("norm2", [P, T, D])
        bn = [sb(f"bn{i}", [P, T, 6]) for i in range(3)]
        mv = [sb(f"mv{i}", [P, T, 2]) for i in range(3)]
        var_eps = [sb(f"var_eps{i}", [P, T]) for i in range(3)]
        minus_mean = [sb(f"minus_mean{i}", [P, T]) for i in range(3)]
        rstd = [[sb(f"rstd{i}_{j}", [P, T]) for j in range(2)] for i in range(3)]
        shift = [[sb(f"shift{i}_{j}", [P, T]) for j in range(2)] for i in range(3)]

        p_hid = [ps(f"p_hid{i}", [P, TN]) for i in range(PF_RING)]
        p_att = ps("p_att", [P, T, N])
        p_pair = [[ps(f"p_pair{i}{b}", [P, T // 2, D]) for b in range(2)] for i in range(2)]

        def ff_banks(s):
            return p_pair[s % 2]

        def nT_banks(s):
            return [p[:].rearrange("p t d -> p (t d)") for p in p_pair[s % 2]]

        def agg_banks(s):
            return p_pair[(s - 1) % 2]

        attn_dma, rows_dma, cols_dma = sem("attn_dma"), sem("rows_dma"), sem("cols_dma")
        w_dma = [sem("w1_dma"), sem("w2_dma")]
        res_rows_ready = sem("res_rows_ready")
        pool_steps = sem("pool_steps")
        w_hi_ready, w_lo_ready = sem("w_hi_ready"), sem("w_lo_ready")
        x_loaded = [sem(f"x_loaded{i}") for i in range(2)]
        adj_loaded = [sem(f"adj_loaded{i}") for i in range(2)]
        x_again_loaded = [sem(f"x_again_loaded{i}") for i in range(2)]
        stored = [sem(f"stored{i}") for i in range(2)]
        mask_steps = sem("mask_steps")
        x0_ready = sem("x0_ready")
        dots_ready = sem("dots_ready")
        sj_rows_ready = sem("sj_rows_ready")
        score_steps = sem("score_steps")
        probs_ready = sem("probs_ready")
        sum_steps = sem("sum_steps")
        pT_psum = sem("pT_psum")
        pT_hi_ready = sem("pT_hi_ready")
        pT_lo_ready = sem("pT_lo_ready")
        X_hi_ready = sem("X_hi_ready")
        X_lo_ready = sem("X_lo_ready")
        agg_ready = sem("agg_ready")
        res1_ready = sem("res1_ready")
        stat_steps = [sem(f"stat_steps{i}") for i in range(3)]
        rstd_ready = [sem(f"rstd_ready{i}") for i in range(3)]
        norm1_ready = sem("norm1_ready")
        nT_psum = sem("nT_psum")
        hT_ready = sem("hT_ready")
        hT_hi_ready = sem("hT_hi_ready")
        hT_lo_ready = sem("hT_lo_ready")
        h_res_steps = sem("h_res_steps")
        hid_psum = sem("hid_psum")
        gelu_ready = sem("gelu_ready")
        g_hi_ready = sem("g_hi_ready")
        g_lo_ready = sem("g_lo_ready")
        ff_done = sem("ff_done")
        res2_ready = sem("res2_ready")
        norm2_ready = sem("norm2_ready")
        x_steps = sem("x_steps")

        def piece(l, n):
            half = slice(n % 2, n % 2 + 1) if n < 2 else slice(C // 2 * (n % 2), C // 2 * (n % 2 + 1))
            return [w[:, half, :] for w in ((w1_f32, w1_hi[l], w1_lo[l]) if n < 2 else (w2_f32, w2_hi[l], w2_lo[l]))]

        pieces = [(l, n) for l in range(L) for n in range(4)]
        act_pieces = dict(zip([(-2, 2), (-2, 4), (-1, 0), (-1, 1)] + [(s, c) for s in range(4) for c in (0, 1)], pieces))
        dve_pieces = dict(zip([(-2, 5), (-1, 2), (-1, 5), (-1, 6)] + [(s, c) for s in range(3) for c in (5, 6)] + [(3, 2), (3, 3)], pieces))

        block = ctx.enter_context(nc.Block())

        @block.sync
        def _(sp):
            def weights(l):
                if l >= 1:
                    sp.wait_ge(w_lo_ready, 4 * l - 2)
                sp.dma_start(w1_f32[:], W1[l].rearrange("(k p) h -> p k h", p=P)).then_inc(w_dma[0], 16)
                if l >= 1:
                    sp.wait_ge(w_lo_ready, 4 * l)
                sp.dma_start(w2_f32[:], W2[l].rearrange("(c p) d -> p c d", p=P)).then_inc(w_dma[1], 16)

            def graphs(tensor, g):
                v = tensor.rearrange("(g t) n d -> n g t d", t=T)
                if isinstance(g, int):
                    return v[:, g]
                return v[:, bass.ds(g, 1)].rearrange("n g t d -> n (g t) d")

            def load_x(g, i):
                sp.dma_start(x_in[i][:], graphs(x, g)).then_inc(x_loaded[i], 16)

            def load_adj(g, i):
                sp.dma_start(adj_in[i][:], graphs(adj, g)).then_inc(adj_loaded[i], 16)

            def load_again(g, i):
                sp.dma_start(x_again[i][:], graphs(x, g)).then_inc(x_again_loaded[i], 16)

            def store(g, i):
                sp.dma_start(graphs(out, g), y_out[i][:]).then_inc(stored[i], 16)

            load_x(0, 0)
            load_adj(0, 0)
            flat = lambda v: v.rearrange("l d -> (l d)")
            sp.dma_start(attn_rows[:].rearrange("p l a d -> p (l a d)"),
                         flat(attn_w).partition_broadcast(P)).then_inc(attn_dma, 16)
            sp.dma_start(attn_b_col[:], attn_b.partition_broadcast(P)).then_inc(attn_dma, 16)
            load_x(1, 1)
            load_adj(1, 1)
            weights(0)
            for g in (2, 3, 4, 5):
                sp.wait_ge(x0_ready, 4 * (g - 1))
                load_x(g, g % 2)
                sp.wait_ge(mask_steps, 2 * (g - 1))
                load_adj(g, g % 2)
                if g == 2:
                    for dst, v in ((g1_rows, g1), (b2_rows, b2), (res_rows, beta1), (g2_rows, g2), (beta2_rows, beta2)):
                        sp.dma_start(dst[:].rearrange("p l d -> p (l d)"),
                                     flat(v).partition_broadcast(P)).then_inc(rows_dma, 16)
                    for dst, v in ((b1_col, b1), (g1_col, g1), (beta1_col, beta1)):
                        with nc.allow_non_contiguous_dma("a feature per partition, once"):
                            sp.dma_start(dst[:], v.rearrange("l (c p) -> p l c", p=P)).then_inc(cols_dma, 16)
                if g in (3, 4):
                    weights(g - RING + 2)
            load_again(0, 0)
            load_again(1, 1)
            with sp.Fori(0, LOOPS - 1) as r:
                for q in range(RING):
                    i, g = q % 2, r * RING + q
                    sp.wait_ge(x0_ready, r * (4 * RING) + 4 * (RING + q + 1))
                    load_x(g + (RING + 2), i)
                    sp.wait_ge(mask_steps, r * (2 * RING) + 2 * (RING + q + 1))
                    load_adj(g + (RING + 2), i)
                    sp.wait_ge(x_steps, x_total(r, 2 * RING + q, 5))
                    store(g, i)
                    load_again(g + 2, i)
            for g in range(RING * (LOOPS - 1), G):
                if g + RING + 2 < G:
                    sp.wait_ge(x0_ready, 4 * (g + RING + 1))
                    load_x(g + RING + 2, g % 2)
                    sp.wait_ge(mask_steps, 2 * (g + RING + 1))
                    load_adj(g + RING + 2, g % 2)
                sp.wait_ge(x_steps, x_total(g // RING, 2 * RING + g % RING, 5))
                store(g, g % 2)
                if g + 2 < G:
                    load_again(g + 2, g % 2)
            for i in range(2):
                sp.wait_ge(stored[i], 16 * G // 2)

        @block.tensor
        def _(pe):
            def hidden(r, s, c):
                l, i = layer_of(s), s % 2
                if c == 0:
                    pe.wait_ge(hT_hi_ready, total(r, s, 1, 1))
                if later(r, s) or c >= PF_RING:
                    pe.wait_ge(gelu_ready, total(r, s, C, c + 1 - PF_RING))
                cols = slice(c * P, (c + 1) * P)
                for n, (w, h, k) in enumerate((w, h, k) for w, h in ((w1_hi, hT_hi), (w1_lo, hT_hi), (w1_hi, hT_lo))
                                              for k in range(KD)):
                    if c == 0 and n == 2 * KD:
                        pe.wait_ge(hT_lo_ready, total(r, s, 1, 1))
                    mm = pe.matmul(p_hid[in_ring(s, c, PF_RING)][:], w[l][:, k, cols], h[i][:, k, :],
                                   start=(n == 0), stop=(n == 3 * KD - 1))
                mm.then_inc(hid_psum, 1)

            def feed(r, s, c):
                l, i = layer_of(s), in_ring(s, c, GS_RING)
                if c == 0 and is_item(r, s + 1):
                    pe.wait_ge(res1_ready, total(r, s + 1, 4, 4))
                pe.wait_ge(g_hi_ready, total(r, s, C, c + 1))
                pe.wait_ge(g_lo_ready, total(r, s, C, c + 1))
                for t in range(T):
                    nodes = slice(t * N, (t + 1) * N)
                    for n, (g, w) in enumerate(((g_hi, w2_hi), (g_hi, w2_lo), (g_lo, w2_hi))):
                        mm = pe.matmul(ff_banks(s)[t // 2][:, t % 2, :], g[i][:, nodes], w[l][:, c, :],
                                       start=(c == 0 and t % 2 == 0 and n == 0),
                                       stop=(c == C - 1 and n == 2), skip_group_check=True)
                mm.then_inc(ff_done, 1)

            def spread_sj(r, s):
                pe.wait_ge(dots_ready, total(r, s, 8, 8))
                if later(r, s):
                    pe.wait_ge(pT_lo_ready, total(r, s - 1, 1, 1))
                for t in range(T):
                    mm = pe.transpose(p_att[:, t, :], s_j[s % RING][:, t:t + 1].broadcast_to([P, P]), ident[:])
                mm.then_inc(sj_rows_ready, 1)

            def transpose_probs(r, s):
                pe.wait_ge(probs_ready, total(r, s, 1, 1))
                for t in range(T):
                    mm = pe.transpose(p_att[:, t, :], probs[:, t, :], ident[:])
                mm.then_inc(pT_psum, 1)

            def aggregate(r, s):
                pe.wait_ge(pT_lo_ready, total(r, s, 1, 1))
                pe.wait_ge(X_lo_ready, total(r, s, 1, 1))
                if later(r, s):
                    pe.wait_ge(hT_ready, total(r, s - 1, 2, 2))
                for t in range(T):
                    nodes = slice(t * N, (t + 1) * N)
                    for n, (p, v) in enumerate(((pT_hi, X_hi), (pT_hi, X_lo), (pT_lo, X_hi))):
                        mm = pe.matmul(agg_banks(s)[t // 2][:, t % 2, :], p[:, nodes], v[:, t, :],
                                       start=(n == 0), stop=(n == 2))
                mm.then_inc(agg_ready, 1)

            def transpose_norm1(r, s):
                if later(r, s, 2):
                    pe.wait_ge(res2_ready, total(r, s - 2, 2, 2))
                pe.wait_ge(norm1_ready, total(r, s, 4, 4))
                for k in range(KD):
                    for t in range(T):
                        mm = pe.transpose(nT_banks(s)[k][:, t * N:(t + 1) * N],
                                          norm1[:, t, k * P:(k + 1) * P], ident[:])
                    mm.then_inc(nT_psum, 1)

            def slot(r, s):
                for c in range(C):
                    if isinstance(r, int) and r == 0 and (s, c) in ((0, 0), (0, LAG), (3, C - 1)):
                        pe.wait_ge(w_lo_ready, {(0, 0): 2, (0, LAG): 4, (3, C - 1): 4 * L}[s, c])
                    if is_item(r, s):
                        hidden(r, s, c)
                    if c == 7 and is_item(r, s + 2):
                        transpose_probs(r, s + 2)
                    if c < LAG and is_item(r, s - 1):
                        feed(r, s - 1, C - LAG + c)
                    if c >= LAG and is_item(r, s):
                        feed(r, s, c - LAG)
                    first = isinstance(r, int) and r == 0 and s in (-2, -1)
                    if c == 4 and first:
                        spread_sj(r, s + 2)
                    if c == 4 and is_item(r, s + 1):
                        transpose_norm1(r, s + 1)
                    if c == 4 and is_item(r, s + 2) and not first:
                        spread_sj(r, s + 2)
                    if c == 0 and is_item(r, s + 1):
                        aggregate(r, s + 1)

            pe.wait_ge(pool_steps, 4)
            slots(pe, slot)

        @block.scalar
        def _(act):
            def high_weights(l, n):
                w, hi, _ = piece(l, n)
                act.wait_ge(w_dma[n // 2], 16 * (l + 1))
                act.activation(hi, w, ACT.Copy, scale=WSCALE).then_inc(w_hi_ready, 1)

            def hidden(r, s, c):
                g, i, k = (in_ring(s, c, n) for n in (G32_RING, GS_RING, PF_RING))
                act.wait_ge(hid_psum, total(r, s, C, c + 1))
                if later(r, s) or c >= G32_RING:
                    act.wait_ge(g_lo_ready, total(r, s, C, c + 1 - G32_RING))
                l = layer_of(s)
                act.activation(g32[g][:], p_hid[k][:], ACT.Gelu, bias=b1_col[:, l, c:c + 1],
                               scale=1.0 / WSCALE).then_inc(gelu_ready, 1)
                act.wait_ge(gelu_ready, total(r, s, C, c + 1))
                if later(r, s) or c >= GS_RING:
                    act.wait_ge(ff_done, total(r, s, C, c + 1 - GS_RING))
                act.activation(g_hi[i][:], g32[g][:], ACT.Copy).then_inc(g_hi_ready, 1)

            def norm_apply(s, n, src, dst, func, done):
                for t in range(T):
                    act.activation(dst[:, t, :], src[:, t, :], func, bias=shift[n][s % 2][:, t:t + 1],
                                   scale=rstd[n][s % 2][:, t:t + 1]).then_inc(done, 1)

            def norm_input(r, s):
                act.wait_ge(rstd_ready[0], group_total(r, s, 2, 2))
                norm_apply(s, 0, x_in[s % 2], X[s % RING], ACT.Relu, x0_ready)

            def norm_attention(r, s):
                act.wait_ge(rstd_ready[1], total(r, s, 2, 2))
                if later(r, s):
                    act.wait_ge(nT_psum, total(r, s - 1, 2, 2))
                    act.wait_ge(h_res_steps, total(r, s - 1, 2, 2))
                norm_apply(s, 1, res1, norm1, ACT.Identity, norm1_ready)

            def norm_feed(r, s):
                act.wait_ge(rstd_ready[2], total(r, s, 2, 2))
                if later(r, s):
                    act.wait_ge(x_steps, x_total(r, s - 1, 3))
                norm_apply(s, 2, res2, norm2, ACT.Identity, norm2_ready)

            def exponentials(r, s):
                act.wait_ge(score_steps, total(r, s, 5, 5))
                act.activation(probs[:], scores[:], ACT.Exp).then_inc(probs_ready, 1)

            def copy_probs(r, s):
                act.wait_ge(pT_psum, total(r, s, 1, 1))
                act.activation(pT_hi[:], p_att[:].rearrange("p t n -> p (t n)"), ACT.Copy).then_inc(pT_hi_ready, 1)

            def high_X(r, s):
                if layer_of(s) == 0:
                    act.wait_ge(x0_ready, group_total(r, s, 4, 4))
                else:
                    act.wait_ge(x_steps, x_total(r, s - RING, 4))
                if later(r, s):
                    act.wait_ge(agg_ready, total(r, s - 1, 1, 1))
                act.activation(X_hi[:], X[s % RING][:], ACT.Copy).then_inc(X_hi_ready, 1)

            def scale_hT(r, s):
                l = layer_of(s)
                if later(r, s):
                    act.wait_ge(hT_lo_ready, total(r, s - 1, 1, 1))
                for k in range(KD):
                    act.wait_ge(nT_psum, total(r, s, 2, k + 1))
                    act.activation(hT[:, k, :], nT_banks(s)[k], ACT.Identity, bias=beta1_col[:, l, k:k + 1],
                                   scale=g1_col[:, l, k:k + 1]).then_inc(hT_ready, 1)
                act.wait_ge(hT_ready, total(r, s, 2, 2))
                if later(r, s, 2):
                    act.wait_ge(hid_psum, total(r, s - 2, C, C))
                act.activation(hT_hi[s % 2][:], hT[:], ACT.Copy).then_inc(hT_hi_ready, 1)

            def slot(r, s):
                if isinstance(r, int) and (r, s) == (0, -1):
                    act.wait_ge(cols_dma, 3 * 16)
                for c in range(C):
                    if isinstance(r, int) and r == 0 and (s, c) in act_pieces:
                        high_weights(*act_pieces[s, c])
                    if is_item(r, s):
                        hidden(r, s, c)
                    if c == 2 and is_item(r, s + 1):
                        norm_attention(r, s + 1)
                    if c == 3 and is_item(r, s + 2):
                        high_X(r, s + 2)
                    if c == 4 and is_item(r, s + 1):
                        scale_hT(r, s + 1)
                    if c == 5 and is_item(r, s + 2):
                        exponentials(r, s + 2)
                    if c == 6 and is_item(r, s + 2):
                        copy_probs(r, s + 2)
                    if c == 6 and is_item(r, s - 1):
                        norm_feed(r, s - 1)
                    if c == 7 and is_item(r, s + 3) and layer_of(s + 3) == 0:
                        norm_input(r, s + 3)

            slots(act, slot)

        @block.vector
        def _(dve):
            def low_weights(l, n):
                w, hi, lo = piece(l, n)
                dve.wait_ge(w_hi_ready, 4 * l + n + 1)
                dve.scalar_tensor_tensor(out=lo, in0=w, scalar=WSCALE, in1=hi,
                                         op0=ALU.mult, op1=ALU.subtract).then_inc(w_lo_ready, 1)

            def hidden(r, s, c):
                g, i = in_ring(s, c, G32_RING), in_ring(s, c, GS_RING)
                dve.wait_ge(g_hi_ready, total(r, s, C, c + 1))
                dve.tensor_tensor(g_lo[i][:], g32[g][:], g_hi[i][:], ALU.subtract).then_inc(g_lo_ready, 1)

            def statistics(n, src):
                for t in range(T):
                    dve.bn_stats(bn[n][:, t, :], src[:, t, :]).then_inc(stat_steps[n], 1)

            def aggregates(n, after_8):
                for t in range(T):
                    dve.bn_aggr(mv[n][:, t, :], bn[n][:, t, :]).then_inc(stat_steps[n], 1)
                dve.wait_ge(stat_steps[n], after_8)
                dve.tensor_scalar(var_eps[n][:], mv[n][:, :, 1], EPS, None, ALU.add).then_inc(stat_steps[n], 1)
                dve.tensor_scalar(minus_mean[n][:], mv[n][:, :, 0], -1.0, None, ALU.mult).then_inc(stat_steps[n], 1)

            def input_statistics(r, s):
                dve.wait_ge(x_loaded[s % 2], lane_total(r, s))
                if later(r, s):
                    dve.wait_ge(rstd_ready[0], group_total(r, s, 2, 0))
                statistics(0, x_in[s % 2])

            def make_mask(r, s):
                a = adj_in[s % 2]
                dve.wait_ge(pool_steps, 5)
                dve.wait_ge(adj_loaded[s % 2], lane_total(r, s))
                dve.tensor_tensor(a[:], a[:], eye_i[:].unsqueeze(1).broadcast_to([P, T, N]),
                                  ALU.add).then_inc(mask_steps, 1)
                dve.wait_ge(mask_steps, group_total(r, s, 2, 1))
                dve.tensor_scalar(mask[s % RING][:], a[:], 0.0, MASKED, ALU.is_le, ALU.mult).then_inc(mask_steps, 1)

            def dot_products(r, s, pair):
                l, q = layer_of(s), s % RING
                if l == 0:
                    dve.wait_ge(x0_ready, group_total(r, s, 4, 2 * pair + 2))
                else:
                    dve.wait_ge(x_steps, x_total(r, s - RING, 2 * pair + 2))
                for t in (2 * pair, 2 * pair + 1):
                    dve.tensor_tensor_reduce(out=dots[:, 2 * t, :], in0=X[q][:, t, :], in1=attn_rows[:, l, 0, :], scale=1.0,
                                             scalar=attn_b_col[:, l:l + 1], op0=ALU.mult, op1=ALU.add,
                                             accum_out=s_i[q][:, t:t + 1]).then_inc(dots_ready, 1)
                    dve.tensor_tensor_reduce(out=dots[:, 2 * t + 1, :], in0=X[q][:, t, :], in1=attn_rows[:, l, 1, :], scale=1.0,
                                             scalar=0.0, op0=ALU.mult, op1=ALU.add,
                                             accum_out=s_j[q][:, t:t + 1]).then_inc(dots_ready, 1)

            def add_scores(r, s):
                q = s % RING
                dve.wait_ge(sj_rows_ready, total(r, s, 1, 1))
                dve.tensor_tensor(leaky[:], p_att[:], mask[q][:], ALU.add).then_inc(score_steps, 1)
                dve.wait_ge(score_steps, total(r, s, 5, 1))
                dve.wait_ge(dots_ready, total(r, s, 8, 8))
                dve.tensor_tensor(scores[:], leaky[:], s_i[q][:].unsqueeze(2).broadcast_to([P, T, N]),
                                  ALU.add).then_inc(score_steps, 1)

            def leaky_scores(r, s):
                dve.wait_ge(score_steps, total(r, s, 5, 2))
                dve.scalar_tensor_tensor(out=leaky[:], in0=scores[:], scalar=SLOPE, in1=scores[:],
                                         op0=ALU.mult, op1=ALU.max).then_inc(score_steps, 1)

            def shift_scores(r, s):
                dve.wait_ge(score_steps, total(r, s, 5, 3))
                dve.tensor_reduce(row_max[:], leaky[:], AX.X, ALU.max).then_inc(score_steps, 1)
                dve.wait_ge(score_steps, total(r, s, 5, 4))
                dve.tensor_tensor(scores[:], leaky[:], row_max[:].unsqueeze(2).broadcast_to([P, T, N]),
                                  ALU.subtract).then_inc(score_steps, 1)

            def row_sums(r, s):
                dve.wait_ge(probs_ready, total(r, s, 1, 1))
                dve.tensor_reduce(row_sum[:], probs[:], AX.X, ALU.add).then_inc(sum_steps, 1)
                dve.wait_ge(sum_steps, total(r, s, 2, 1))
                dve.reciprocal(row_inv[:], row_sum[:]).then_inc(sum_steps, 1)

            def attention_residual(r, s):
                dve.wait_ge(agg_ready, total(r, s, 1, 1))
                dve.wait_ge(sum_steps, total(r, s, 2, 2))
                if later(r, s):
                    dve.wait_ge(norm1_ready, total(r, s - 1, 4, 4))
                for t in range(T):
                    dve.scalar_tensor_tensor(out=res1[:, t, :], in0=agg_banks(s)[t // 2][:, t % 2, :],
                                             scalar=row_inv[:, t:t + 1], in1=X[s % RING][:, t, :],
                                             op0=ALU.mult, op1=ALU.add).then_inc(res1_ready, 1)

            def attention_statistics(r, s):
                dve.wait_ge(res1_ready, total(r, s, 4, 4))
                statistics(1, res1)

            def low_probs(r, s):
                dve.wait_ge(pT_hi_ready, total(r, s, 1, 1))
                dve.tensor_tensor(pT_lo[:], p_att[:].rearrange("p t n -> p (t n)"), pT_hi[:],
                                  ALU.subtract).then_inc(pT_lo_ready, 1)

            def split_hT(r, s):
                dve.wait_ge(hT_hi_ready, total(r, s, 1, 1))
                dve.tensor_tensor(hT_lo[s % 2][:], hT[:], hT_hi[s % 2][:], ALU.subtract).then_inc(hT_lo_ready, 1)

            def feed_residual(r, s):
                dve.wait_ge(ff_done, total(r, s, C, C))
                dve.wait_ge(h_res_steps, total(r, s, 2, 2))
                if later(r, s):
                    dve.wait_ge(norm2_ready, total(r, s - 1, 4, 4))
                for b in range(2):
                    pair = slice(2 * b, 2 * b + 2)
                    dve.scalar_tensor_tensor(out=res2[:, pair, :], in0=ff_banks(s)[b][:], scalar=1.0 / WSCALE,
                                             in1=h_res[s % 2][:, pair, :],
                                             op0=ALU.mult, op1=ALU.add).then_inc(res2_ready, 1)

            def feed_statistics(r, s):
                dve.wait_ge(res2_ready, total(r, s, 2, 2))
                statistics(2, res2)

            def last_output(r, s):
                y = y_out[s % 2]
                dve.wait_ge(x_steps, x_total(r, s, 0))
                dve.wait_ge(stored[s % 2], 16 * (G // 2 - 1))
                dve.wait_ge(x_again_loaded[s % 2], 16 * G // 2)
                for p in range(2):
                    pair = slice(2 * p, 2 * p + 2)
                    g2_pair, beta2_pair = (v[:, L - 1, :].unsqueeze(1).broadcast_to([P, 2, D])
                                           for v in (g2_rows, beta2_rows))
                    dve.wait_ge(norm2_ready, total(r, s, 4, 2 * p + 2))
                    dve.tensor_tensor(y[:, pair, :], norm2[:, pair, :], g2_pair, ALU.mult).then_inc(x_steps, 1)
                    dve.wait_ge(x_steps, x_total(r, s, 2 * p + 1))
                    dve.tensor_tensor(y[:, pair, :], y[:, pair, :], beta2_pair, ALU.add).then_inc(x_steps, 1)
                dve.wait_ge(x_steps, x_total(r, s, 4))
                dve.tensor_tensor(y[:], y[:], x_again[s % 2][:], ALU.add).then_inc(x_steps, 1)

            def slot(r, s):
                starts = is_item(r, s + 4) and layer_of(s + 4) == 0
                late = isinstance(r, int) and (r, s) == (0, -3)
                if isinstance(r, int) and (r, s) == (0, -2):
                    dve.wait_ge(attn_dma, 2 * 16)
                for c in range(C):
                    if c == 0 and is_item(r, s + 1):
                        dve.wait_ge(stat_steps[1], total(r, s + 1, 10, 4))
                    if c == 4 and is_item(r, s - 1):
                        dve.wait_ge(stat_steps[2], total(r, s - 1, 10, 4))
                    if c == 6 and starts and not late:
                        dve.wait_ge(stat_steps[0], group_total(r, s + 4, 10, 4))
                    if isinstance(r, int) and (r, s, c) == (0, -2, 3):
                        dve.wait_ge(stat_steps[0], group_total(0, 1, 10, 4))
                    if is_item(r, s):
                        hidden(r, s, c)
                    if c == 0 and is_item(r, s + 1):
                        aggregates(1, total(r, s + 1, 10, 8))
                    if c == 2 and is_item(r, s - 1):
                        feed_residual(r, s - 1)
                    if c in (1, 2) and is_item(r, s + 2):
                        dot_products(r, s + 2, c // 2)
                    if isinstance(r, int) and (r, s, c) == (0, -2, 2):
                        input_statistics(0, 1)
                    if isinstance(r, int) and (r, s, c) == (0, -2, 3):
                        aggregates(0, group_total(0, 1, 10, 8))
                    if c == 3 and is_item(r, s - 1):
                        feed_statistics(r, s - 1)
                    if c == 4 and is_item(r, s + 2):
                        add_scores(r, s + 2)
                        leaky_scores(r, s + 2)
                        shift_scores(r, s + 2)
                    if c == 4 and is_item(r, s - 1):
                        aggregates(2, total(r, s - 1, 10, 8))
                    if c == 5 and is_item(r, s + 1):
                        split_hT(r, s + 1)
                    if c == 5 and starts and not late:
                        input_statistics(r, s + 4)
                    if c == 6 and is_item(r, s + 2):
                        low_probs(r, s + 2)
                    if c == 6 and starts and not late:
                        aggregates(0, group_total(r, s + 4, 10, 8))
                    if c == 6 and is_item(r, s + 2):
                        row_sums(r, s + 2)
                    if c == 6 and starts:
                        make_mask(r, s + 4)
                    if c == 7 and is_item(r, s + 2):
                        attention_residual(r, s + 2)
                        attention_statistics(r, s + 2)
                    if isinstance(r, int) and r == 0 and (s, c) in dve_pieces:
                        low_weights(*dve_pieces[s, c])
                    if isinstance(r, int) and (r, s, c) == (0, -1, 0):
                        dve.wait_ge(rows_dma, 5 * 16)
                        dve.tensor_tensor(res_rows[:], res_rows[:], b2_rows[:], ALU.add).then_inc(res_rows_ready, 1)

            slots(dve, slot)
            last_output(LOOPS, PER - 1)

        @block.gpsimd
        def _(pool):
            pool.memset(ident[:], 0.0).then_inc(pool_steps, 1)
            pool.memset(eye_i[:], 0).then_inc(pool_steps, 1)
            pool.memset(minus_half[:], -0.5).then_inc(pool_steps, 1)
            pool.wait_ge(pool_steps, 3)
            pool.affine_select(out=ident[:], in_=ident[:], compare_op=ALU.not_equal, fill=1.0, base=0,
                               pattern=[[-1, P]], channel_multiplier=1).then_inc(pool_steps, 1)
            pool.wait_ge(pool_steps, 4)
            pool.tensor_copy(eye_i[:], ident[:]).then_inc(pool_steps, 1)

            def rows(v, l, graphs=2):
                return v[:, l, :].unsqueeze(1).broadcast_to([P, graphs, D])

            def inverse_deviation(s, n, count_stats, count_rstd):
                pool.wait_ge(stat_steps[n], count_stats)
                pool.tensor_tensor(rstd[n][s % 2][:], var_eps[n][:], minus_half[:], ALU.pow).then_inc(rstd_ready[n], 1)
                pool.wait_ge(rstd_ready[n], count_rstd)
                pool.tensor_tensor(shift[n][s % 2][:], minus_mean[n][:], rstd[n][s % 2][:], ALU.mult).then_inc(rstd_ready[n], 1)

            def h_residual(r, s):
                l, i = layer_of(s), s % 2
                pool.wait_ge(norm1_ready, total(r, s, 4, 4))
                if later(r, s, 2):
                    pool.wait_ge(res2_ready, total(r, s - 2, 2, 2))
                pool.tensor_tensor(h_res[i][:], norm1[:], rows(g1_rows, l, T), ALU.mult).then_inc(h_res_steps, 1)
                pool.wait_ge(h_res_steps, total(r, s, 2, 1))
                pool.tensor_tensor(h_res[i][:], h_res[i][:], rows(res_rows, l, T), ALU.add).then_inc(h_res_steps, 1)

            def low_X(r, s):
                pool.wait_ge(X_hi_ready, total(r, s, 1, 1))
                pool.tensor_tensor(X_lo[:], X[s % RING][:], X_hi[:], ALU.subtract).then_inc(X_lo_ready, 1)

            def layer_output(r, s):
                l, q = layer_of(s), s % RING
                dst = y_out[q % 2] if l == L - 1 else X[q]
                if l == L - 1 and later(r, s, 2 * RING + 2):
                    pool.wait_ge(stored[q % 2], stored_total(r, q))
                for p in range(2):
                    pair = slice(2 * p, 2 * p + 2)
                    pool.wait_ge(norm2_ready, total(r, s, 4, 2 * p + 2))
                    pool.tensor_tensor(dst[:, pair, :], norm2[:, pair, :], rows(g2_rows, l), ALU.mult).then_inc(x_steps, 1)
                    pool.wait_ge(x_steps, x_total(r, s, 2 * p + 1))
                    pool.tensor_tensor(dst[:, pair, :], dst[:, pair, :], rows(beta2_rows, l), ALU.add).then_inc(x_steps, 1)

            def skip_connection(r, s):
                i = s % 2
                pool.wait_ge(x_steps, x_total(r, s, 4))
                pool.wait_ge(x_again_loaded[i], lane_total(r, s - 2 * RING))
                pool.tensor_tensor(y_out[i][:], y_out[i][:], x_again[i][:], ALU.add).then_inc(x_steps, 1)

            def slot(r, s):
                if isinstance(r, int) and (r, s) == (0, -1):
                    pool.wait_ge(rows_dma, 5 * 16)
                    pool.wait_ge(res_rows_ready, 1)
                if is_item(r, s + 1):
                    inverse_deviation(s + 1, 1, total(r, s + 1, 10, 10), total(r, s + 1, 2, 1))
                    h_residual(r, s + 1)
                if is_item(r, s + 2):
                    low_X(r, s + 2)
                if is_item(r, s - 1):
                    inverse_deviation(s - 1, 2, total(r, s - 1, 10, 10), total(r, s - 1, 2, 1))
                if is_item(r, s - 2) and layer_of(s - 2) == L - 1:
                    skip_connection(r, s - 2)
                if is_item(r, s + 4) and layer_of(s + 4) == 0:
                    inverse_deviation(s + 4, 0, group_total(r, s + 4, 10, 10), group_total(r, s + 4, 2, 1))
                if is_item(r, s - 1) and not (isinstance(r, int) and PER * r + s == ITEMS):
                    layer_output(r, s - 1)

            slots(pool, slot)

    return nc


INPUTS = ["x", "adj", "L0_gnn_attn_w", "L0_gnn_attn_b", "L0_gnn_W1", "L0_gnn_b1", "L0_gnn_W2", "L0_gnn_b2",
          "L0_gnn_g1", "L0_gnn_beta1", "L0_gnn_g2", "L0_gnn_beta2"]


def kernel(**inputs):
    import concourse.bacc as bacc
    from concourse.bass_utils import run_bass_kernel_spmd

    nc = bacc.Bacc("TRN2", target_bir_lowering=False, num_devices=1)
    arrays, args = {}, []
    for name in INPUTS:
        a = np.ascontiguousarray(inputs[name])
        arrays[f"in_{name}"] = a
        args.append(nc.dram_tensor(f"in_{name}", a.shape, mybir.dt.from_np(a.dtype), kind="ExternalInput").ap())
    out = nc.dram_tensor("out_0", (B, N, D), F32, kind="ExternalOutput").ap()
    gnn_kernel(nc, *args, out)
    return run_bass_kernel_spmd(nc, [arrays], core_ids=[0]).results[0]["out_0"]
```
